# Optimizing a Trainium2 kernel written in Bass

```python
import numpy as np
import jax
import jax.numpy as jnp

def _softmax(x, axis=-1):
    return jax.nn.softmax(x, axis=axis)

def _gelu(x):
    return jax.nn.gelu(x, approximate=True)

def _silu(x):
    return jax.nn.silu(x)

def _sigmoid(x):
    return jax.nn.sigmoid(x)

def _layernorm(x, axis=-1, eps=1e-05):
    m = jnp.mean(x, axis=axis, keepdims=True)
    v = jnp.var(x, axis=axis, keepdims=True)
    return (x - m) / jnp.sqrt(v + eps)

def _scatter_add(tgt, idx, src, axis=0):
    return tgt.at[idx].add(src)

def _segment_sum(src, seg, n):
    return jax.ops.segment_sum(src, seg, n)
kernel_name = 'mk_adaln_d1_jaxref_r8_c17eb3'

def setup_inputs(seed: int=0):
    np.random.seed(seed)
    _w = jnp.asarray

    def _L0_attn_setup():
        import jax, jax.numpy as jnp
        import numpy as np
        D_MODEL = 256
        N_HEADS = 16
        HEAD_DIM = D_MODEL // N_HEADS
        FF = 1024
        KCONV = 4
        EPS = 1e-05

        def _layernorm(x, w, b, eps=EPS):
            m = jnp.mean(x, axis=-1, keepdims=True)
            v = jnp.mean(jnp.square(x - m), axis=-1, keepdims=True)
            return (x - m) * jax.lax.rsqrt(v + eps) * w + b

        def _long_block(x, Wq, Wk, Wv, Wo, conv_w, conv_b, Wig, big, Wog, bog, Wg, bg, vnw, vnb, mnw, mnb, gnw, gnb, ln1w, ln1b, ln2w, ln2b, Wgate, Wval, Wout):
            B, T, C = x.shape
            H, D = (N_HEADS, HEAD_DIM)
            h = _layernorm(x, ln1w, ln1b)
            ht = jnp.transpose(h, (0, 2, 1))
            xc = jax.lax.conv_general_dilated(ht, conv_w, window_strides=(1,), padding=[(KCONV - 1, 0)], dimension_numbers=('NCH', 'OIH', 'NCH'), feature_group_count=C) + conv_b[None, :, None]
            x_conv = jax.nn.silu(jnp.transpose(xc, (0, 2, 1)))

            def l2norm(t):
                return t * jax.lax.rsqrt(jnp.sum(t * t, axis=-1, keepdims=True) + 1e-12)
            q = l2norm((h @ Wq).reshape(B, T, H, D))
            k = l2norm((h @ Wk).reshape(B, T, H, D))
            v = _layernorm((h @ Wv).reshape(B, T, H, D), vnw, vnb)
            i_gate = jax.nn.sigmoid(x_conv @ Wig + big).reshape(B, T, H, D)
            gamma = jax.nn.sigmoid(x_conv @ Wg + bg).reshape(B, T, H, 1)
            u = i_gate * k * v
            g = jnp.broadcast_to(gamma, u.shape)

            def combine(c1, c2):
                a1, b1 = c1
                a2, b2 = c2
                return (a1 * a2, a2 * b1 + b2)
            _, mem = jax.lax.associative_scan(combine, (g, u), axis=1)
            out = (_layernorm(mem, mnw, mnb) * q).reshape(B, T, C)
            og = out.reshape(B, T, H, D)
            m = jnp.mean(og, axis=-1, keepdims=True)
            var = jnp.mean(jnp.square(og - m), axis=-1, keepdims=True)
            og = (og - m) * jax.lax.rsqrt(var + EPS)
            out = (og * gnw.reshape(H, D) + gnb.reshape(H, D)).reshape(B, T, C)
            out = out * jax.nn.sigmoid(x_conv @ Wog + bog)
            h = x + out @ Wo
            h2 = _layernorm(h, ln2w, ln2b)
            mlp = jax.nn.silu(h2 @ Wgate) * (h2 @ Wval) @ Wout
            return h + mlp
        key = jax.random.key(seed)
        ks = jax.random.split(key, 32)
        B, T = (2, 512)
        s = lambda fan: 1.0 / np.sqrt(fan)
        inp = {'x': jax.random.normal(ks[0], (B, T, D_MODEL), jnp.float32), 'Wq': jax.random.normal(ks[1], (D_MODEL, D_MODEL), jnp.float32) * s(D_MODEL), 'Wk': jax.random.normal(ks[2], (D_MODEL, D_MODEL), jnp.float32) * s(D_MODEL), 'Wv': jax.random.normal(ks[3], (D_MODEL, D_MODEL), jnp.float32) * s(D_MODEL), 'Wo': jax.random.normal(ks[4], (D_MODEL, D_MODEL), jnp.float32) * s(D_MODEL), 'conv_w': jax.random.normal(ks[5], (D_MODEL, 1, KCONV), jnp.float32) * s(KCONV), 'conv_b': jnp.zeros((D_MODEL,), jnp.float32), 'Wig': jnp.zeros((D_MODEL, D_MODEL), jnp.float32), 'big': jnp.full((D_MODEL,), -3.0, jnp.float32), 'Wog': jax.random.normal(ks[6], (D_MODEL, D_MODEL), jnp.float32) * s(D_MODEL), 'bog': jnp.zeros((D_MODEL,), jnp.float32), 'Wg': jnp.zeros((D_MODEL, N_HEADS), jnp.float32), 'bg': jnp.asarray(np.log((lambda d: d / (1.0 - d))(1.0 - np.exp(np.linspace(np.log(1 - 0.9), np.log(1 - 0.999), N_HEADS)))), jnp.float32), 'vnw': jnp.ones((HEAD_DIM,), jnp.float32), 'vnb': jnp.zeros((HEAD_DIM,), jnp.float32), 'mnw': jnp.ones((HEAD_DIM,), jnp.float32), 'mnb': jnp.zeros((HEAD_DIM,), jnp.float32), 'gnw': jnp.ones((D_MODEL,), jnp.float32), 'gnb': jnp.zeros((D_MODEL,), jnp.float32), 'ln1w': jnp.ones((D_MODEL,), jnp.float32), 'ln1b': jnp.zeros((D_MODEL,), jnp.float32), 'ln2w': jnp.ones((D_MODEL,), jnp.float32), 'ln2b': jnp.zeros((D_MODEL,), jnp.float32), 'Wgate': jax.random.normal(ks[7], (D_MODEL, FF), jnp.float32) * s(D_MODEL), 'Wval': jax.random.normal(ks[8], (D_MODEL, FF), jnp.float32) * s(D_MODEL), 'Wout': jax.random.normal(ks[9], (FF, D_MODEL), jnp.float32) * s(FF)}
        return inp
    _L0_attn_in = _L0_attn_setup()

    def _L0_ffn_setup():
        import jax, jax.numpy as jnp
        import numpy as np
        HIDDEN = 256
        FFN = 176
        N_EXPERTS = 16
        TOP_K = 4
        SHARED_FFN = 2 * FFN

        def _glu_ffn(x, gate_up, down):
            gu = x @ gate_up.T
            g, u = jnp.split(gu, 2, axis=-1)
            return jax.nn.silu(g) * u @ down.T
        key = jax.random.key(seed)
        ks = jax.random.split(key, 6)
        s = 0.02
        return {'hidden_states': jax.random.normal(ks[0], (1, 256, HIDDEN), jnp.float32), 'gate_weight': jax.random.normal(ks[1], (N_EXPERTS, HIDDEN), jnp.float32) * s, 'gate_up_weights': jax.random.normal(ks[2], (N_EXPERTS, 2 * FFN, HIDDEN), jnp.float32) * s, 'down_weights': jax.random.normal(ks[3], (N_EXPERTS, HIDDEN, FFN), jnp.float32) * s, 'shared_gate_up': jax.random.normal(ks[4], (2 * SHARED_FFN, HIDDEN), jnp.float32) * s, 'shared_down': jax.random.normal(ks[5], (HIDDEN, SHARED_FFN), jnp.float32) * s}
    _L0_ffn_in = _L0_ffn_setup()
    _L0_c = _w((lambda *s: np.random.randn(*s).astype(np.float32) * 0.05)(2, 256))
    _L0_wmod = _w((lambda *s: np.random.randn(*s).astype(np.float32) * 0.05)(256, 6 * 256) * 256 ** (-0.5))
    _d = {'L0_attn_x': _L0_attn_in['x'], 'L0_attn_Wq': _L0_attn_in['Wq'], 'L0_attn_Wk': _L0_attn_in['Wk'], 'L0_attn_Wv': _L0_attn_in['Wv'], 'L0_attn_Wo': _L0_attn_in['Wo'], 'L0_attn_conv_w': _L0_attn_in['conv_w'], 'L0_attn_conv_b': _L0_attn_in['conv_b'], 'L0_attn_Wig': _L0_attn_in['Wig'], 'L0_attn_big': _L0_attn_in['big'], 'L0_attn_Wog': _L0_attn_in['Wog'], 'L0_attn_bog': _L0_attn_in['bog'], 'L0_attn_Wg': _L0_attn_in['Wg'], 'L0_attn_bg': _L0_attn_in['bg'], 'L0_attn_vnw': _L0_attn_in['vnw'], 'L0_attn_vnb': _L0_attn_in['vnb'], 'L0_attn_mnw': _L0_attn_in['mnw'], 'L0_attn_mnb': _L0_attn_in['mnb'], 'L0_attn_gnw': _L0_attn_in['gnw'], 'L0_attn_gnb': _L0_attn_in['gnb'], 'L0_attn_ln1w': _L0_attn_in['ln1w'], 'L0_attn_ln1b': _L0_attn_in['ln1b'], 'L0_attn_ln2w': _L0_attn_in['ln2w'], 'L0_attn_ln2b': _L0_attn_in['ln2b'], 'L0_attn_Wgate': _L0_attn_in['Wgate'], 'L0_attn_Wval': _L0_attn_in['Wval'], 'L0_attn_Wout': _L0_attn_in['Wout'], 'L0_ffn_gate_weight': _L0_ffn_in['gate_weight'], 'L0_ffn_gate_up_weights': _L0_ffn_in['gate_up_weights'], 'L0_ffn_down_weights': _L0_ffn_in['down_weights'], 'L0_ffn_shared_gate_up': _L0_ffn_in['shared_gate_up'], 'L0_ffn_shared_down': _L0_ffn_in['shared_down'], 'L0_c': _L0_c, 'L0_wmod': _L0_wmod}
    _x0 = _d['L0_attn_x']
    _d['L0_attn_x'] = jax.random.normal(jax.random.fold_in(jax.random.key(seed), 1), (2, 512, 256), dtype=_x0.dtype)
    del _x0
    return _d

def reference(L0_attn_x, L0_attn_Wq, L0_attn_Wk, L0_attn_Wv, L0_attn_Wo, L0_attn_conv_w, L0_attn_conv_b, L0_attn_Wig, L0_attn_big, L0_attn_Wog, L0_attn_bog, L0_attn_Wg, L0_attn_bg, L0_attn_vnw, L0_attn_vnb, L0_attn_mnw, L0_attn_mnb, L0_attn_gnw, L0_attn_gnb, L0_attn_ln1w, L0_attn_ln1b, L0_attn_ln2w, L0_attn_ln2b, L0_attn_Wgate, L0_attn_Wval, L0_attn_Wout, L0_ffn_gate_weight, L0_ffn_gate_up_weights, L0_ffn_down_weights, L0_ffn_shared_gate_up, L0_ffn_shared_down, L0_c, L0_wmod):

    def _L0_attn_ref(x, Wq, Wk, Wv, Wo, conv_w, conv_b, Wig, big, Wog, bog, Wg, bg, vnw, vnb, mnw, mnb, gnw, gnb, ln1w, ln1b, ln2w, ln2b, Wgate, Wval, Wout):
        import jax, jax.numpy as jnp
        import numpy as np
        D_MODEL = 256
        N_HEADS = 16
        HEAD_DIM = D_MODEL // N_HEADS
        FF = 1024
        KCONV = 4
        EPS = 1e-05

        def _layernorm(x, w, b, eps=EPS):
            m = jnp.mean(x, axis=-1, keepdims=True)
            v = jnp.mean(jnp.square(x - m), axis=-1, keepdims=True)
            return (x - m) * jax.lax.rsqrt(v + eps) * w + b

        def _long_block(x, Wq, Wk, Wv, Wo, conv_w, conv_b, Wig, big, Wog, bog, Wg, bg, vnw, vnb, mnw, mnb, gnw, gnb, ln1w, ln1b, ln2w, ln2b, Wgate, Wval, Wout):
            B, T, C = x.shape
            H, D = (N_HEADS, HEAD_DIM)
            h = _layernorm(x, ln1w, ln1b)
            ht = jnp.transpose(h, (0, 2, 1))
            xc = jax.lax.conv_general_dilated(ht, conv_w, window_strides=(1,), padding=[(KCONV - 1, 0)], dimension_numbers=('NCH', 'OIH', 'NCH'), feature_group_count=C) + conv_b[None, :, None]
            x_conv = jax.nn.silu(jnp.transpose(xc, (0, 2, 1)))

            def l2norm(t):
                return t * jax.lax.rsqrt(jnp.sum(t * t, axis=-1, keepdims=True) + 1e-12)
            q = l2norm((h @ Wq).reshape(B, T, H, D))
            k = l2norm((h @ Wk).reshape(B, T, H, D))
            v = _layernorm((h @ Wv).reshape(B, T, H, D), vnw, vnb)
            i_gate = jax.nn.sigmoid(x_conv @ Wig + big).reshape(B, T, H, D)
            gamma = jax.nn.sigmoid(x_conv @ Wg + bg).reshape(B, T, H, 1)
            u = i_gate * k * v
            g = jnp.broadcast_to(gamma, u.shape)

            def combine(c1, c2):
                a1, b1 = c1
                a2, b2 = c2
                return (a1 * a2, a2 * b1 + b2)
            _, mem = jax.lax.associative_scan(combine, (g, u), axis=1)
            out = (_layernorm(mem, mnw, mnb) * q).reshape(B, T, C)
            og = out.reshape(B, T, H, D)
            m = jnp.mean(og, axis=-1, keepdims=True)
            var = jnp.mean(jnp.square(og - m), axis=-1, keepdims=True)
            og = (og - m) * jax.lax.rsqrt(var + EPS)
            out = (og * gnw.reshape(H, D) + gnb.reshape(H, D)).reshape(B, T, C)
            out = out * jax.nn.sigmoid(x_conv @ Wog + bog)
            h = x + out @ Wo
            h2 = _layernorm(h, ln2w, ln2b)
            mlp = jax.nn.silu(h2 @ Wgate) * (h2 @ Wval) @ Wout
            return h + mlp
        return _long_block(x, Wq, Wk, Wv, Wo, conv_w, conv_b, Wig, big, Wog, bog, Wg, bg, vnw, vnb, mnw, mnb, gnw, gnb, ln1w, ln1b, ln2w, ln2b, Wgate, Wval, Wout)

    def _L0_ffn_ref(hidden_states, gate_weight, gate_up_weights, down_weights, shared_gate_up, shared_down):
        import jax, jax.numpy as jnp
        import numpy as np
        HIDDEN = 256
        FFN = 176
        N_EXPERTS = 16
        TOP_K = 4
        SHARED_FFN = 2 * FFN

        def _glu_ffn(x, gate_up, down):
            gu = x @ gate_up.T
            g, u = jnp.split(gu, 2, axis=-1)
            return jax.nn.silu(g) * u @ down.T
        orig_shape = hidden_states.shape
        x = hidden_states.reshape(-1, orig_shape[-1])
        scores = jax.nn.softmax(x @ gate_weight.T, axis=-1)
        topk_weight, topk_idx = jax.lax.top_k(scores, TOP_K)
        y = jnp.zeros_like(x)
        for e in range(N_EXPERTS):
            w_e = jnp.sum(jnp.where(topk_idx == e, topk_weight, 0.0), axis=-1)
            y = y + w_e[:, None] * _glu_ffn(x, gate_up_weights[e], down_weights[e])
        y = y + _glu_ffn(x, shared_gate_up, shared_down)
        return y.reshape(orig_shape)
    x = L0_attn_x
    mod = (_silu(L0_c) @ L0_wmod).reshape(L0_c.shape[0], 6, 1, -1)
    sa, ca, ga, sb, cb, gb = (mod[:, 0], mod[:, 1], mod[:, 2], mod[:, 3], mod[:, 4], mod[:, 5])
    ga = (2 * (ga >= 0) - 1) * jnp.maximum(jnp.abs(ga), 0.25)
    gb = (2 * (gb >= 0) - 1) * jnp.maximum(jnp.abs(gb), 0.25)
    h = _layernorm(x, axis=-1) * (1 + ca) + sa
    x = x + ga * _L0_attn_ref(h, L0_attn_Wq, L0_attn_Wk, L0_attn_Wv, L0_attn_Wo, L0_attn_conv_w, L0_attn_conv_b, L0_attn_Wig, L0_attn_big, L0_attn_Wog, L0_attn_bog, L0_attn_Wg, L0_attn_bg, L0_attn_vnw, L0_attn_vnb, L0_attn_mnw, L0_attn_mnb, L0_attn_gnw, L0_attn_gnb, L0_attn_ln1w, L0_attn_ln1b, L0_attn_ln2w, L0_attn_ln2b, L0_attn_Wgate, L0_attn_Wval, L0_attn_Wout)
    h = _layernorm(x, axis=-1) * (1 + cb) + sb
    x = x + gb * _L0_ffn_ref(h, L0_ffn_gate_weight, L0_ffn_gate_up_weights, L0_ffn_down_weights, L0_ffn_shared_gate_up, L0_ffn_shared_down)
    return x

_drawn_inputs = setup_inputs


def setup_inputs(seed=0):
    import zlib

    import numpy as np

    out = dict(_drawn_inputs(seed))
    spreads = {'L0_attn_conv_b': (0.0, 0.648),
     'L0_attn_Wig': (0.0, 0.1),
     'L0_attn_big': (-3.0, 0.2),
     'L0_attn_bog': (0.0, 0.8),
     'L0_attn_Wg': (0.0, 0.1),
     'L0_attn_vnw': (1.0, 0.2),
     'L0_attn_vnb': (0.0, 0.623),
     'L0_attn_mnw': (1.0, 0.6),
     'L0_attn_mnb': (0.0, 0.545),
     'L0_attn_gnw': (1.0, 0.2),
     'L0_attn_gnb': (0.0, 0.526),
     'L0_attn_ln1w': (1.0, 0.2),
     'L0_attn_ln1b': (0.0, 0.1),
     'L0_attn_ln2w': (1.0, 0.2),
     'L0_attn_ln2b': (0.0, 0.427)}
    factors = {'L0_ffn_gate_weight': 8.0,
     'L0_ffn_gate_up_weights': 8.0,
     'L0_ffn_down_weights': 8.0,
     'L0_ffn_shared_gate_up': 8.0,
     'L0_ffn_shared_down': 8.0}
    for name, (base, spread) in spreads.items():
        noise = np.random.default_rng([zlib.crc32(name.encode()), seed]).standard_normal(out[name].shape)
        drawn = base * np.exp(spread * noise) if base else spread * noise
        out[name] = jnp.asarray(drawn.astype(out[name].dtype))
    for name, factor in factors.items():
        out[name] = (out[name] * factor).astype(out[name].dtype)
    return out
```

```python
import concourse.bass as bass
from concourse import mybir
from contextlib import ExitStack

FP32 = mybir.dt.float32
FP32R = mybir.dt.float32r
BF16 = mybir.dt.bfloat16
ALU = mybir.AluOpType
ACT = mybir.ActivationFunctionType
AX = mybir.AxisListType

P = 128
NB = 2
T = 512
C = 256
KC = C // P
NT = T // P
NH, HD = 16, 16
KCONV = 4
PAD = KCONV - 1
FF = 1024
NF = FF // P
NE, FE = 16, 176
NG = NE + 1
HIDDEN = NE * FE + 2 * FE
NM = -(-HIDDEN // P)
WM = 2 * KC * P + C
TOPK = 4
EPS = 1e-5
LN_HALF = -0.6931471805599453

COLS = ["ln1w", "ln1b", "cw0", "cw1", "cw2", "cw3", "cb", "big", "bg", "bog", "gnw", "gnb", "ln2w", "ln2b"]
ONCE = ["vnw", "vnb", "mnw", "mnb"]
NPAR = 2 * len(COLS) + len(ONCE)
MATS = ["q", "k", "v", "ig", "ga", "og", "o"]

LOG_SET, SILU_SET = "natural_log_exp_and_others", "silu_and_others"


def order():
    both = lambda *names: [(n, b) for n in names for b in range(NB)]
    steps = both("ln0", "qkv", "gates", "stat", "u", "scan", "out", "wo", "ln2")
    for b in range(NB):
        steps += [(f"ff{f}", b) for f in range(NF)] + [("acc", b)]
    return steps + both("ln3", "route")


def adaln_block_kernel(nc, x, cT, wmod, par, wsm, wff, wout, wgate, wmoe, sel, mats, out):
    ctx = ExitStack()
    with ctx:
        def sb(name, shape, dt=FP32):
            return ctx.enter_context(nc.sbuf_tensor(name, shape, dt))

        def sem(name):
            return ctx.enter_context(nc.semaphore(name))

        mats_sb = sb("mats_sb", [P, 3, P])
        ident, blk, cen = (mats_sb[:, i, :] for i in range(3))
        blk_eps = sb("blk_eps", [P, P])
        par_sb = sb("par_sb", [P, NPAR])
        half = sb("half", [P, NPAR])
        wg_sb = sb("wg_sb", [P, KC, NE])
        cT_sb = sb("cT_sb", [P, KC * NB])
        cs = sb("cs", [P, KC * NB])
        cB = sb("cB", [P, KC * NB, P])
        eps_sb = sb("eps_sb", [P, 4])
        mod = sb("mod", [P, NB, 4, C])
        modc = sb("modc", [P, 2 * KC, NB])
        gtmp = sb("gtmp", [P, 2, C])

        wsm_hi = sb("wsm_hi", [P, KC, len(MATS) * C], FP32R)
        wsm_lo = sb("wsm_lo", [P, KC, len(MATS) * C], FP32R)
        wff_hi = sb("wff_hi", [P, KC, 2 * FF], FP32R)
        wff_lo = sb("wff_lo", [P, KC, 2 * FF], FP32R)
        wout_hi = sb("wout_hi", [P, NF, C], FP32R)
        wout_lo = sb("wout_lo", [P, NF, C], FP32R)
        stage = sb("stage", [P, 2, 1024])
        sel_bf = sb("sel_bf", [3 * NG, NM * P], BF16)
        zeros = sb("zeros", [P, T], BF16)
        vmean = sb("vmean", [P, KC * NH])

        hm = [sb(f"hm{b}", [P, NT, C]) for b in range(NB)]
        hpad = [sb(f"hpad{b}", [P, KC, PAD + T]) for b in range(NB)]
        W = [[sb(f"w{b}_{i}", [P, KC, T]) for i in range(7)] for b in range(NB)]
        a_hi = [sb(f"a_hi{b}", [P, KC, T], FP32R) for b in range(NB)]
        a_lo = [sb(f"a_lo{b}", [P, KC, T], FP32R) for b in range(NB)]
        b_hi = [sb(f"b_hi{b}", [P, KC, T], FP32R) for b in range(NB)]
        b_lo = [sb(f"b_lo{b}", [P, KC, T], FP32R) for b in range(NB)]
        st = [sb(f"st{b}", [P, NT, 6]) for b in range(NB)]
        mv = [sb(f"mv{b}", [P, NT, 2]) for b in range(NB)]
        rr = [sb(f"rr{b}", [P, NT]) for b in range(NB)]
        top8 = [sb(f"top8{b}", [P, NT, 8]) for b in range(NB)]
        sc = [sb(f"sc{b}", [P, NT, NE + 4]) for b in range(NB)]
        rep = [sb(f"rep{b}", [P, NT, NE + 4]) for b in range(NB)]
        sums = [sb(f"sums{b}", [P, NT]) for b in range(NB)]
        wres = [sb(f"wres{b}", [P, NT, NE]) for b in range(NB)]
        wb = [sb(f"wb{b}", [P, 3, NT, NE], BF16) for b in range(NB)]
        wcat = [sb(f"wcat{b}", [P, NT, 3 * NG]) for b in range(NB)]
        wT = sb("wT", [3 * NG, NB, T], BF16)

        PS = [ctx.enter_context(nc.psum_tensor(f"ps{i}", [P, 2, T], FP32)) for i in range(4)]
        PA = lambda b: PS[2 * b]
        PB = lambda b: PS[2 * b + 1]
        tok = lambda ps: ps[:, :, :].rearrange("p a (t c) -> p (a t) c", c=C)

        wmod_raw = [W[0][2 + i] for i in range(3)]
        wsm_raw = [W[1][3 + i] for i in range(4)]

        def col(name, c=0, of=None):
            j = 2 * COLS.index(name) + c if name in COLS else 2 * len(COLS) + ONCE.index(name)
            return (par_sb if of is None else of)[:, j:j + 1]

        def mat(w, name, k, m):
            o = MATS.index(name) * C + m * P
            return w[:, k, o:o + P]

        f32 = lambda ap: ap.bitcast(FP32)

        S = {}

        def s(name):
            return S[name]

        for name in (
            "cT_in par_in mats_in wg_in wmod_in x_again out_done "
            "cs_ready cB_ready eps_ready par_half blk_eps_ready "
            "mod_shift mod_gate mod_chan mod_used modt_ready modg_ready modc_ready "
            "vsum_ready wsm_ready chunk_split "
            "var0 rstd0 var1 rstd1 hn_ready t1_ready h1_full h1_used h1_lo "
            "q_psum q_used k_psum k_used v_psum v_used conv_ready x_full x_hi x_lo "
            "ig_psum ig_tanh ga_psum ga_tanh og_psum og_tanh a1_done gamma_ready "
            "ssk_psum ssk_used rk_ready ssv_psum ssv_used rv_ready u_ready uc_psum mem_ready "
            "sqm_ready ssm_psum ssm_used rm_ready o1_ready oc_psum sqo_ready oc_used vo_psum vo_used ro_ready "
            "gated out_hi out_lo wo_psum wo_sb tw_psum tw_used var2 rstd2 hn2_ready t2_psum h2_used h2_full h2_lo "
            "g_psum v2_psum silu_done prod_done hid_hi hid_lo down_done acc_sb tm_psum tm_used "
            "var3 rstd3 hn3_ready t3_psum h3_used h3_full h3_lo lg_psum lg_sub exp_done wcat_ready wt_psum wt_ready "
            "dve_order act_order pool_order moe_hi moe_ready0 moe_ready1 zeros_ready "
            "mg_psum mu_psum mw_psum msilu mprod mgated mhi mlo mdown macc_sb mt_psum y_ready"
        ).split():
            S[name] = sem(name)
        x_in = [sem(f"x_in{b}") for b in range(NB)]
        stage_in = [sem(f"stage_in{i}") for i in range(2)]
        wsm_in = [sem(f"wsm_in{i}") for i in range(4)]
        raw_in = [sem(f"raw_in{i}") for i in range(2)]

        CH = [("ff", i) for i in range(4)] + [("out", i) for i in range(2)] + [("sel", i) for i in range(-(-NM // 8))]

        def raw_slot(j):
            return W[1][4 + j][:, :, :].rearrange("p a n -> p (a n)")[:, 0:WM]

        def mw(w, j):
            return w[:, 0, j * WM:(j + 1) * WM]

        def mgu(w, j, k, which):
            o = j * WM + (2 * k + which) * P
            return w[:, 0, o:o + P]

        def mdn(w, j, m):
            o = j * WM + 2 * KC * P + m * P
            return w[:, 0, o:o + P]

        block = ctx.enter_context(nc.Block())

        @block.sync
        def _(sp):
            sp.dma_start(W[0][0][:, :, :].rearrange("p a (t c) -> p (a t) c", c=C),
                         x[0:T, :].rearrange("(t p) c -> p t c", p=P)).then_inc(x_in[0], 16)
            sp.dma_start(cT_sb[:, :], cT).then_inc(s("cT_in"), 16)
            for i in range(3):
                sp.dma_start(wmod_raw[i][:, :, :], wmod[:, :, i * T:(i + 1) * T]).then_inc(s("wmod_in"), 16)
            sp.dma_start(mats_sb[:, :, :], mats).then_inc(s("mats_in"), 16)
            sp.dma_start(par_sb[:, :], par).then_inc(s("par_in"), 16)
            for i in range(4):
                n = min(2 * C, len(MATS) * C - i * 2 * C)
                sp.dma_start(wsm_raw[i][:, :, 0:n], wsm[:, :, i * 2 * C:i * 2 * C + n]).then_inc(wsm_in[i], 16)
                if i == 0:
                    sp.dma_start(W[1][0][:, :, :].rearrange("p a (t c) -> p (a t) c", c=C),
                                 x[T:2 * T, :].rearrange("(t p) c -> p t c", p=P)).then_inc(x_in[1], 16)
            sp.dma_start(wg_sb[:, :, :], wgate).then_inc(s("wg_in"), 16)
            for n, (kind, i) in enumerate(CH):
                if n >= 2:
                    sp.wait_ge(s("chunk_split"), n - 1)
                slot = stage[:, n % 2, :]
                if kind == "ff":
                    sp.dma_start(slot.rearrange("p (k n) -> p k n", k=KC),
                                 wff[:, :, i * 512:(i + 1) * 512]).then_inc(stage_in[n % 2], 16)
                elif kind == "out":
                    sp.dma_start(slot.rearrange("p (f n) -> p f n", n=C),
                                 wout[:, 4 * i:4 * i + 4, :]).then_inc(stage_in[n % 2], 16)
                else:
                    w = min(1024, NM * P - i * 1024)
                    sp.dma_start(slot[0:3 * NG, 0:w], sel[:, i * 1024:i * 1024 + w]).then_inc(stage_in[n % 2], 16)
            for b in range(NB):
                sp.wait_ge(s("gated"), b + 1)
                if b:
                    sp.wait_ge(s("x_again"), 16)
                sp.dma_start(W[b][0][:, :, :].rearrange("p a (t c) -> p (a t) c", c=C),
                             x[b * T:(b + 1) * T, :].rearrange("(t p) c -> p t c", p=P)).then_inc(s("x_again"), 16)
            sp.wait_ge(s("vo_psum"), NB)
            sp.wait_ge(s("o1_ready"), NB)
            for j in range(2):
                sp.dma_start(raw_slot(j), wmoe[j, :, :]).then_inc(raw_in[j], 16)
            with sp.Fori(0, (NM - 3) // 2) as it:
                for j in range(2):
                    sp.wait_ge(s("moe_ready" + str(j)), it + 1)
                    sp.dma_start(raw_slot(j), wmoe[it * 2 + j + 2, :, :]).then_inc(raw_in[j], 16)
            sp.wait_ge(s("moe_ready0"), (NM - 1) // 2)
            sp.dma_start(raw_slot(0), wmoe[NM - 1, :, :]).then_inc(raw_in[0], 16)
            for b in range(NB):
                sp.wait_ge(s("y_ready"), b + 1)
                sp.dma_start(out[b * T:(b + 1) * T, :].rearrange("(t p) c -> p t c", p=P),
                             hm[b][:, :, :]).then_inc(s("out_done"), 16)
            sp.wait_ge(s("out_done"), 16 * NB)

        @block.gpsimd
        def _(pool):
            n = [0]

            def done(ins):
                ins.then_inc(s("pool_order"), 1)
                n[0] += 1
                return n[0]

            def split(hi, lo, raw):
                at = done(nc.gpsimd.tensor_scalar(hi, raw, 1.0, None, ALU.mult))
                pool.wait_ge(s("pool_order"), at)
                return nc.gpsimd.tensor_tensor(lo, raw, f32(hi), ALU.subtract)

            for i, v in enumerate((EPS, 1e-12, EPS * 1e-12, LN_HALF)):
                last = nc.gpsimd.memset(eps_sb[:, i:i + 1], v)
            last.then_inc(s("eps_ready"), 1)
            for b in range(NB):
                w4 = wcat[b][:, :, :].rearrange("p t (g e) -> p t g e", e=NG)
                nc.gpsimd.memset(w4[:, :, 1:3, NE:NG], 0.0)
                nc.gpsimd.memset(w4[:, :, 0, NE:NG], 1.0)
                for i in range(4):
                    nc.gpsimd.memset(sc[b][:, :, NE + i:NE + i + 1], -5.0 - i)
                last = nc.gpsimd.memset(hpad[b][:, :, 0:PAD], 0.0)
            last.then_inc(s("eps_ready"), 1)
            nc.gpsimd.memset(zeros[:, :], 0.0).then_inc(s("zeros_ready"), 1)
            for m, name in enumerate(MATS):
                raw = wsm_raw[m // 2][:, :, (m % 2) * C:(m % 2 + 1) * C]
                pool.wait_ge(wsm_in[m // 2], 16)
                if name == "v":
                    g = raw.rearrange("p k (h d) -> p k h d", d=HD)
                    vm = vmean[:, :].rearrange("p (k h) -> p k h", k=KC)
                    pool.wait_ge(s("vsum_ready"), 1)
                    at = done(nc.gpsimd.tensor_scalar(vmean[:, :], vmean[:, :], 1.0 / HD, None, ALU.mult))
                    pool.wait_ge(s("pool_order"), at)
                    for k in range(KC):
                        at = done(nc.gpsimd.tensor_tensor(g[:, k], g[:, k],
                                                          vm[:, k].unsqueeze(2).broadcast_to([P, NH, HD]),
                                                          ALU.subtract))
                    pool.wait_ge(s("pool_order"), at)
                split(wsm_hi[:, :, m * C:(m + 1) * C], wsm_lo[:, :, m * C:(m + 1) * C], raw).then_inc(s("wsm_ready"), 1)
            for c, (kind, i) in enumerate(CH):
                pool.wait_ge(stage_in[c % 2], 16 * (c // 2 + 1))
                slot = stage[:, c % 2, :]
                if kind == "ff":
                    raw = slot.rearrange("p (k n) -> p k n", k=KC)
                    ins = split(wff_hi[:, :, i * 512:(i + 1) * 512], wff_lo[:, :, i * 512:(i + 1) * 512], raw)
                elif kind == "out":
                    raw = slot.rearrange("p (f n) -> p f n", n=C)
                    ins = split(wout_hi[:, 4 * i:4 * i + 4, :], wout_lo[:, 4 * i:4 * i + 4, :], raw)
                else:
                    w = min(1024, NM * P - i * 1024)
                    ins = nc.gpsimd.tensor_scalar(sel_bf[:, i * 1024:i * 1024 + w], slot[0:3 * NG, 0:w],
                                                  1.0, None, ALU.mult)
                ins.then_inc(s("chunk_split"), 1)
            def moe_low(j):
                nc.gpsimd.tensor_tensor(mw(wsm_lo, j), raw_slot(j), f32(mw(wsm_hi, j)),
                                        ALU.subtract).then_inc(s("moe_ready" + str(j)), 1)

            for j in range(2):
                pool.wait_ge(s("moe_hi"), j + 1)
                moe_low(j)
            with pool.Fori(0, (NM - 3) // 2) as it:
                for j in range(2):
                    pool.wait_ge(s("moe_hi"), it * 2 + j + 3)
                    moe_low(j)
            pool.wait_ge(s("moe_hi"), NM)
            moe_low(0)

        @block.scalar
        def _(act):
            n = [0]
            loaded = [None]

            def done(ins):
                ins.then_inc(s("act_order"), 1)
                n[0] += 1
                act.wait_ge(s("act_order"), n[0])

            def table(name):
                if loaded[0] != name:
                    nc.scalar.preload_act_table_set(name)
                    loaded[0] = name

            eps, tiny, epstiny, lnhalf = (eps_sb[:, i:i + 1] for i in range(4))

            def rsqrt(out, in_, bias, scale=1.0, bias2=0.0):
                table(LOG_SET)
                first = nc.scalar.activation(out, in_, ACT.Ln, bias=bias, scale=scale)
                done(first)
                return nc.scalar.activation(out, out, ACT.Exp, scale=-0.5, bias=bias2)

            table(SILU_SET)
            act.wait_ge(s("cT_in"), 16)
            nc.scalar.activation(cs[:, :], cT_sb[:, :], ACT.Silu).then_inc(s("cs_ready"), 1)
            act.wait_ge(s("eps_ready"), 2)

            def small_rstd(b, var, rstd):
                act.wait_ge(s(var), b + 1)
                rsqrt(rr[b][:, :], mv[b][:, :, 1], eps).then_inc(s(rstd), 1)

            def ln0(b):
                small_rstd(b, "var0", "rstd0")
                small_rstd(b, "var1", "rstd1")
                act.wait_ge(s("par_in"), 16)
                act.wait_ge(s("t1_ready"), b + 1)
                for c in range(KC):
                    nc.scalar.activation(a_hi[b][:, c, :], PB(b)[:, c, :], ACT.Identity,
                                         scale=col("ln1w", c), bias=col("ln1b", c))
                    last = nc.scalar.activation(hpad[b][:, c, PAD:PAD + T], PB(b)[:, c, :], ACT.Identity,
                                                scale=col("ln1w", c), bias=col("ln1b", c))
                last.then_inc(s("h1_full"), 1)

            def qkv(b):
                act.wait_ge(s("q_psum"), b + 1)
                nc.scalar.activation(W[b][1][:, :, :], PA(b)[:, :, :], ACT.Copy)
                act.wait_ge(s("mod_gate"), NB)
                if b == 1:
                    act.wait_ge(s("wsm_ready"), len(MATS))
                nc.scalar.activation(W[b][4][:, :, :], PA(b)[:, :, :], ACT.Square).then_inc(s("q_used"), 1)
                act.wait_ge(s("k_psum"), b + 1)
                nc.scalar.activation(W[b][2][:, :, :], PB(b)[:, :, :], ACT.Copy)
                nc.scalar.activation(W[b][5][:, :, :], PB(b)[:, :, :], ACT.Square).then_inc(s("k_used"), 1)
                table(SILU_SET)
                act.wait_ge(s("conv_ready"), b + 1)
                done(nc.scalar.activation(W[b][0][:, :, :], W[b][0][:, :, :], ACT.Silu))
                nc.scalar.activation(b_hi[b][:, :, :], W[b][0][:, :, :], ACT.Copy).then_inc(s("x_hi"), 1)
                act.wait_ge(s("v_psum"), b + 1)
                nc.scalar.activation(W[b][3][:, :, :], PA(b)[:, :, :], ACT.Copy)
                nc.scalar.activation(W[b][6][:, :, :], PA(b)[:, :, :], ACT.Square).then_inc(s("v_used"), 1)

            def tanh_half(dst, ps, bias, ready):
                table(SILU_SET)
                for c in range(KC):
                    last = nc.scalar.activation(dst[:, c, :], ps[:, c, :], ACT.Tanh, scale=0.5,
                                                bias=col(bias, c, of=half))
                last.then_inc(s(ready), 1)

            def gates(b):
                act.wait_ge(s("par_half"), 1)
                act.wait_ge(s("ig_psum"), b + 1)
                act.wait_ge(s("x_lo"), b + 1)
                tanh_half(W[b][0], PB(b), "big", "ig_tanh")
                act.wait_ge(s("ga_psum"), b + 1)
                tanh_half(hpad[b][:, :, 0:T], PA(b), "bg", "ga_tanh")
                act.wait_ge(s("og_psum"), b + 1)
                act.wait_ge(s("a1_done"), b + 1)
                tanh_half(W[b][0], PA(b), "bog", "og_tanh")

            def stat(b):
                act.wait_ge(s("ssk_psum"), b + 1)
                rsqrt(W[b][5][:, :, :], PB(b)[:, :, :], tiny, scale=float(HD), bias2=lnhalf).then_inc(s("rk_ready"), 1)
                act.wait_ge(s("ssv_psum"), b + 1)
                rsqrt(W[b][6][:, :, :], PA(b)[:, :, :], eps).then_inc(s("rv_ready"), 1)

            def scan(b):
                act.wait_ge(s("mem_ready"), b + 1)
                nc.scalar.activation(W[b][5][:, :, :], W[b][3][:, :, :], ACT.Square).then_inc(s("sqm_ready"), 1)
                act.wait_ge(s("ssm_psum"), b + 1)
                rsqrt(W[b][5][:, :, :], PA(b)[:, :, :], eps).then_inc(s("rm_ready"), 1)
                act.wait_ge(s("oc_psum"), b + 1)
                nc.scalar.activation(W[b][6][:, :, :], PB(b)[:, :, :], ACT.Square).then_inc(s("sqo_ready"), 1)

            def out_(b):
                act.wait_ge(s("vo_psum"), b + 1)
                rsqrt(W[b][6][:, :, :], PA(b)[:, :, :], epstiny).then_inc(s("ro_ready"), 1)
                act.wait_ge(s("gated"), b + 1)
                nc.scalar.activation(a_hi[b][:, :, :], W[b][2][:, :, :], ACT.Copy).then_inc(s("out_hi"), 1)

            def wo(b):
                act.wait_ge(s("wo_psum"), b + 1)
                nc.scalar.activation(W[b][3][:, :, :], PA(b)[:, :, :], ACT.Copy).then_inc(s("wo_sb"), 1)

            def ln2(b):
                small_rstd(b, "var2", "rstd2")
                act.wait_ge(s("t2_psum"), b + 1)
                for c in range(KC):
                    nc.scalar.activation(b_hi[b][:, c, :], PA(b)[:, c, :], ACT.Identity,
                                         scale=col("ln2w", c), bias=col("ln2b", c))
                    last = nc.scalar.activation(W[b][3][:, c, :], PA(b)[:, c, :], ACT.Identity,
                                                scale=col("ln2w", c), bias=col("ln2b", c))
                last.then_inc(s("h2_full"), 1)

            def ff_silu(b, f):
                u = b * NF + f
                table(SILU_SET)
                act.wait_ge(s("g_psum"), u + 1)
                nc.scalar.activation(W[b][1][:, f % 2, :], PA(b)[:, 0, :], ACT.Silu).then_inc(s("silu_done"), 1)

            def ff_hi(b, f):
                u = b * NF + f
                act.wait_ge(s("prod_done"), u + 1)
                if f >= 2:
                    act.wait_ge(s("down_done"), u - 1)
                nc.scalar.activation(a_hi[b][:, f % 2, :], W[b][2][:, f % 2, :], ACT.Copy).then_inc(s("hid_hi"), 1)

            def ff(b, f):
                ff_silu(b, f)
                ff_hi(b, f)

            def acc(b):
                act.wait_ge(s("down_done"), (b + 1) * NF)
                act.wait_ge(s("h2_lo"), b + 1)
                nc.scalar.activation(W[b][3][:, :, :], PB(b)[:, :, :], ACT.Copy).then_inc(s("acc_sb"), 1)

            def ln3(b):
                small_rstd(b, "var3", "rstd3")
                act.wait_ge(s("modc_ready"), 1)
                act.wait_ge(s("t3_psum"), b + 1)
                for c in range(KC):
                    nc.scalar.activation(b_hi[b][:, c, :], PB(b)[:, c, :], ACT.Identity,
                                         scale=modc[:, KC + c, b:b + 1], bias=modc[:, c, b:b + 1])
                    last = nc.scalar.activation(W[b][3][:, c, :], PB(b)[:, c, :], ACT.Identity,
                                                scale=modc[:, KC + c, b:b + 1], bias=modc[:, c, b:b + 1])
                last.then_inc(s("h3_full"), 1)

            def route(b):
                table(LOG_SET)
                act.wait_ge(s("lg_sub"), b + 1)
                nc.scalar.activation(rep[b][:, :, 0:NE], rep[b][:, :, 0:NE], ACT.Exp).then_inc(s("exp_done"), 1)

            steps = {"ln0": ln0, "qkv": qkv, "gates": gates, "stat": stat, "scan": scan, "out": out_, "wo": wo,
                     "ln2": ln2, "acc": acc, "ln3": ln3, "route": route}
            for name, b in order():
                if name[:2] == "ff":
                    ff(b, int(name[2:]))
                elif name in steps:
                    steps[name](b)

            def weights_high(j):
                nc.scalar.activation(mw(wsm_hi, j), raw_slot(j), ACT.Copy).then_inc(s("moe_hi"), 1)

            def moe(b, at):
                act.wait_ge(s("mg_psum"), at + b + 1)
                nc.scalar.activation(W[0][1][:, b, :], PS[2][:, 0, :], ACT.Silu).then_inc(s("msilu"), 1)
                act.wait_ge(s("mgated"), at + b + 1)
                if not isinstance(at, int) or at:
                    act.wait_ge(s("mdown"), at + b - 1)
                nc.scalar.activation(a_hi[0][:, b, :], W[0][3][:, b, :], ACT.Copy).then_inc(s("mhi"), 1)

            def moe_tiles(it, last=False):
                for jj in range(2):
                    moe(0, it * 4 + 2 * jj + 2)
                    if not (last and jj == 1):
                        act.wait_ge(raw_in[jj], it * 16 + 32)
                        act.wait_ge(s("mdown"), it * 4 + 2 * jj + 2)
                        weights_high(jj)
                    moe(1, it * 4 + 2 * jj + 2)

            table(SILU_SET)
            act.wait_ge(s("wo_psum"), NB)
            for j in range(2):
                act.wait_ge(raw_in[j], 16)
                weights_high(j)
            for b in range(NB):
                moe(b, 0)
            with act.Fori(0, (NM - 3) // 2) as it:
                moe_tiles(it)
            moe_tiles((NM - 3) // 2, last=True)
            for b in range(NB):
                act.wait_ge(s("mdown"), 2 * NM + b)
                nc.scalar.activation(W[b][0][:, :, :], PS[b][:, :, :], ACT.Copy).then_inc(s("macc_sb"), 1)

        @block.vector
        def _(dve):
            n = [0]

            def done(ins):
                ins.then_inc(s("dve_order"), 1)
                n[0] += 1
                return n[0]

            def link(ins):
                dve.wait_ge(s("dve_order"), done(ins))

            def stats(b, rows, ready):
                for t in range(NT):
                    at = done(nc.vector.bn_stats(st[b][:, t, :], rows[:, t, :]))
                dve.wait_ge(s("dve_order"), at)
                for t in range(NT):
                    last = nc.vector.bn_aggr(mv[b][:, t, :], st[b][:, t, :])
                last.then_inc(s(ready), 1)

            def normalise(b, dst, rows, ready):
                for t in range(NT):
                    last = nc.vector.tensor_scalar(dst[:, t, :], rows[:, t, :], mv[b][:, t, 0:1], rr[b][:, t:t + 1],
                                                   ALU.subtract, ALU.mult)
                return last

            def per_token(b, i):
                return mod[:, b, i, :].unsqueeze(1).broadcast_to([P, NT, C])

            dve.wait_ge(s("eps_ready"), 2)
            dve.wait_ge(s("cs_ready"), 1)
            nc.vector.tensor_copy(cB[:, :, :], cs[:, :].unsqueeze(2).broadcast_to([P, KC * NB, P])).then_inc(s("cB_ready"), 1)
            dve.wait_ge(s("par_in"), 16)
            nc.vector.tensor_scalar(half[:, :], par_sb[:, :], 0.5, None, ALU.mult).then_inc(s("par_half"), 1)
            dve.wait_ge(s("mats_in"), 16)
            nc.vector.tensor_scalar(blk_eps[:, :], blk, EPS * HD, None, ALU.mult).then_inc(s("blk_eps_ready"), 1)

            def shift_scale(b):
                dve.wait_ge(s("mod_shift"), b + 1)
                nc.vector.tensor_copy(mod[:, b, 0, :], PA(b)[:, 0, 0:C])
                link(nc.vector.tensor_scalar(mod[:, b, 1, :], PA(b)[:, 0, C:2 * C], 1.0, None, ALU.add))

            def gate_mod(b):
                dve.wait_ge(s("mod_gate"), b + 1)
                if b == 0:
                    dve.wait_ge(s("mod_chan"), 1)
                    nc.vector.tensor_copy(modc[:, 0:KC, :], PB(0)[:, 0, 0:KC * NB].rearrange("p (j b) -> p j b", b=NB))
                    nc.vector.tensor_scalar(modc[:, KC:2 * KC, :],
                                            PB(0)[:, 0, KC * NB:2 * KC * NB].rearrange("p (j b) -> p j b", b=NB),
                                            1.0, None, ALU.add).then_inc(s("modc_ready"), 1)
                g = PA(b)[:, 1, :].rearrange("p (j c) -> p j c", c=C)
                link(nc.vector.tensor_scalar(gtmp[:, :, :], g, 0.0, 2.0, ALU.is_ge, ALU.mult))
                link(nc.vector.tensor_scalar(gtmp[:, :, :], gtmp[:, :, :], -1.0, None, ALU.add))
                link(nc.vector.tensor_tensor(mod[:, b, 2:4, :], gtmp[:, :, :], g, ALU.mult))
                nc.vector.scalar_tensor_tensor(mod[:, b, 2:4, :], mod[:, b, 2:4, :], 0.25, gtmp[:, :, :],
                                               ALU.max, ALU.mult).then_inc(s("mod_used"), 1)

            def ln0(b):
                xt, hn = tok(W[b][0]), tok(W[b][1])
                dve.wait_ge(x_in[b], 16)
                stats(b, xt, "var0")
                shift_scale(b)
                dve.wait_ge(s("rstd0"), b + 1)
                link(normalise(b, hn, xt, None))
                link(nc.vector.tensor_tensor(hm[b][:, :, :], hn, per_token(b, 1), ALU.mult))
                link(nc.vector.tensor_tensor(hm[b][:, :, :], hm[b][:, :, :], per_token(b, 0), ALU.add))
                stats(b, hm[b], "var1")
                gate_mod(b)
                if b == 0:
                    dve.wait_ge(wsm_in[1], 16)
                    vw = wsm_raw[1][:, :, 0:C].rearrange("p k (h d) -> p k h d", d=HD)
                    nc.vector.tensor_reduce(vmean[:, :].rearrange("p (k h) -> p k h", k=KC), vw,
                                            AX.X, ALU.add).then_inc(s("vsum_ready"), 1)
                dve.wait_ge(s("rstd1"), b + 1)
                normalise(b, hn, hm[b], None).then_inc(s("hn_ready"), 1)

            def qkv(b):
                dve.wait_ge(s("h1_full"), b + 1)
                nc.vector.tensor_tensor(a_lo[b][:, :, :], hpad[b][:, :, PAD:PAD + T], f32(a_hi[b][:, :, :]),
                                        ALU.subtract).then_inc(s("h1_lo"), 1)
                written = [0] * KC
                for k in range(KCONV):
                    for c in range(KC):
                        if k:
                            dve.wait_ge(s("dve_order"), written[c])
                        src = hpad[b][:, c, k:k + T]
                        if k == 0:
                            ins = nc.vector.tensor_scalar(W[b][0][:, c, :], src, col("cw0", c), col("cb", c),
                                                          ALU.mult, ALU.add)
                        else:
                            ins = nc.vector.scalar_tensor_tensor(W[b][0][:, c, :], src, col(f"cw{k}", c),
                                                                 W[b][0][:, c, :], ALU.mult, ALU.add)
                        if k == KCONV - 1 and c == KC - 1:
                            ins.then_inc(s("conv_ready"), 1)
                        else:
                            written[c] = done(ins)
                dve.wait_ge(s("x_hi"), b + 1)
                nc.vector.tensor_tensor(b_lo[b][:, :, :], W[b][0][:, :, :], f32(b_hi[b][:, :, :]),
                                        ALU.subtract).then_inc(s("x_lo"), 1)

            def gates(b):
                dve.wait_ge(s("ig_tanh"), b + 1)
                dve.wait_ge(s("k_used"), b + 1)
                nc.vector.scalar_tensor_tensor(W[b][2][:, :, :], W[b][0][:, :, :], 1.0, W[b][2][:, :, :],
                                               ALU.add, ALU.mult).then_inc(s("a1_done"), 1)
                dve.wait_ge(s("ga_tanh"), b + 1)
                nc.vector.tensor_scalar(hpad[b][:, :, 0:T], hpad[b][:, :, 0:T], 0.5, 0.5,
                                        ALU.mult, ALU.add).then_inc(s("gamma_ready"), 1)

            def u(b):
                dve.wait_ge(s("rk_ready"), b + 1)
                dve.wait_ge(s("a1_done"), b + 1)
                done(nc.vector.tensor_tensor(W[b][2][:, :, :], W[b][2][:, :, :], W[b][5][:, :, :], ALU.mult))
                dve.wait_ge(s("rv_ready"), b + 1)
                link(nc.vector.scalar_tensor_tensor(W[b][3][:, :, :], W[b][3][:, :, :], col("vnw"), W[b][6][:, :, :],
                                                    ALU.mult, ALU.mult))
                nc.vector.scalar_tensor_tensor(W[b][3][:, :, :], W[b][3][:, :, :], col("vnb"), W[b][2][:, :, :],
                                               ALU.add, ALU.mult).then_inc(s("u_ready"), 1)

            def scan(b):
                dve.wait_ge(s("uc_psum"), b + 1)
                dve.wait_ge(s("gamma_ready"), b + 1)
                for c in range(KC):
                    last = nc.vector.tensor_tensor_scan(W[b][3][:, c, :], hpad[b][:, c, 0:T], PB(b)[:, c, :], 0.0,
                                                        ALU.mult, ALU.add)
                last.then_inc(s("mem_ready"), 1)
                dve.wait_ge(s("rm_ready"), b + 1)
                link(nc.vector.scalar_tensor_tensor(W[b][3][:, :, :], W[b][3][:, :, :], col("mnw"), W[b][5][:, :, :],
                                                    ALU.mult, ALU.mult))
                nc.vector.scalar_tensor_tensor(W[b][3][:, :, :], W[b][3][:, :, :], col("mnb"), W[b][1][:, :, :],
                                               ALU.add, ALU.mult).then_inc(s("o1_ready"), 1)

            def out_(b):
                dve.wait_ge(s("og_tanh"), b + 1)
                done(nc.vector.tensor_scalar(W[b][0][:, :, :], W[b][0][:, :, :], 0.5, 0.5, ALU.mult, ALU.add))
                dve.wait_ge(s("ro_ready"), b + 1)
                for c in range(KC):
                    at = done(nc.vector.scalar_tensor_tensor(W[b][2][:, c, :], PB(b)[:, c, :], col("gnw", c),
                                                             W[b][6][:, c, :], ALU.mult, ALU.mult))
                dve.wait_ge(s("dve_order"), at)
                for c in range(KC):
                    last = nc.vector.scalar_tensor_tensor(W[b][2][:, c, :], W[b][2][:, c, :], col("gnb", c),
                                                          W[b][0][:, c, :], ALU.add, ALU.mult)
                last.then_inc(s("gated"), 1)
                dve.wait_ge(s("out_hi"), b + 1)
                nc.vector.tensor_tensor(a_lo[b][:, :, :], W[b][2][:, :, :], f32(a_hi[b][:, :, :]),
                                        ALU.subtract).then_inc(s("out_lo"), 1)

            def wo(b):
                dve.wait_ge(s("tw_psum"), b + 1)
                nc.vector.tensor_tensor(hm[b][:, :, :], hm[b][:, :, :], tok(PB(b)), ALU.add).then_inc(s("tw_used"), 1)
                dve.wait_ge(s("tw_used"), b + 1)
                stats(b, hm[b], "var2")

            def ln2(b):
                dve.wait_ge(s("rstd2"), b + 1)
                normalise(b, tok(W[b][1]), hm[b], None).then_inc(s("hn2_ready"), 1)
                dve.wait_ge(s("h2_full"), b + 1)
                nc.vector.tensor_tensor(b_lo[b][:, :, :], W[b][3][:, :, :], f32(b_hi[b][:, :, :]),
                                        ALU.subtract).then_inc(s("h2_lo"), 1)

            def ff(b, f):
                i = b * NF + f
                dve.wait_ge(s("v2_psum"), i + 1)
                dve.wait_ge(s("silu_done"), i + 1)
                nc.vector.tensor_tensor(W[b][2][:, f % 2, :], W[b][1][:, f % 2, :], PA(b)[:, 1, :],
                                        ALU.mult).then_inc(s("prod_done"), 1)
                dve.wait_ge(s("hid_hi"), i + 1)
                nc.vector.tensor_tensor(a_lo[b][:, f % 2, :], W[b][2][:, f % 2, :], f32(a_hi[b][:, f % 2, :]),
                                        ALU.subtract).then_inc(s("hid_lo"), 1)

            def ln3(b):
                dve.wait_ge(s("tm_psum"), b + 1)
                nc.vector.tensor_tensor(hm[b][:, :, :], hm[b][:, :, :], tok(PA(b)), ALU.add).then_inc(s("tm_used"), 1)
                dve.wait_ge(s("tm_used"), b + 1)
                dve.wait_ge(s("mod_used"), NB)
                link(nc.vector.tensor_tensor(hm[b][:, :, :], hm[b][:, :, :], per_token(b, 2), ALU.mult))
                dve.wait_ge(s("x_again"), 16 * (b + 1))
                link(nc.vector.tensor_tensor(hm[b][:, :, :], hm[b][:, :, :], tok(W[b][0]), ALU.add))
                stats(b, hm[b], "var3")
                dve.wait_ge(s("rstd3"), b + 1)
                normalise(b, tok(W[b][1]), hm[b], None).then_inc(s("hn3_ready"), 1)
                dve.wait_ge(s("h3_full"), b + 1)
                nc.vector.tensor_tensor(b_lo[b][:, :, :], W[b][3][:, :, :], f32(b_hi[b][:, :, :]),
                                        ALU.subtract).then_inc(s("h3_lo"), 1)

            def route(b):
                lg = tok(PA(b))[:, :, 0:NE]
                dve.wait_ge(s("lg_psum"), b + 1)
                for t in range(NT):
                    at = done(nc.vector.max(top8[b][:, t, :], lg[:, t, :]))
                dve.wait_ge(s("dve_order"), at)
                nc.vector.tensor_tensor(rep[b][:, :, 0:NE], lg, top8[b][:, :, 0:1].broadcast_to([P, NT, NE]),
                                        ALU.subtract).then_inc(s("lg_sub"), 1)
                dve.wait_ge(s("exp_done"), b + 1)
                link(nc.vector.tensor_reduce(sums[b][:, :], rep[b][:, :, 0:NE], AX.X, ALU.add))
                link(nc.vector.reciprocal(sums[b][:, :], sums[b][:, :]))
                link(nc.vector.tensor_tensor(sc[b][:, :, 0:NE], rep[b][:, :, 0:NE],
                                             sums[b][:, :].unsqueeze(2).broadcast_to([P, NT, NE]), ALU.mult))
                for t in range(NT):
                    at = done(nc.vector.max(top8[b][:, t, :], sc[b][:, t, 0:NE]))
                dve.wait_ge(s("dve_order"), at)
                link(nc.vector.tensor_copy(top8[b][:, :, TOPK:8], sc[b][:, :, NE:NE + 4]))
                for t in range(NT):
                    at = done(nc.vector.match_replace(rep[b][:, t, :], top8[b][:, t, :], sc[b][:, t, :], -1.0))
                dve.wait_ge(s("dve_order"), at)
                link(nc.vector.scalar_tensor_tensor(wres[b][:, :, :], rep[b][:, :, 0:NE], 0.0, sc[b][:, :, 0:NE],
                                                    ALU.is_lt, ALU.mult))
                w4 = wcat[b][:, :, :].rearrange("p t (g e) -> p t g e", e=NG)
                for g in range(3):
                    link(nc.vector.tensor_copy(wb[b][:, g, :, :], wres[b][:, :, :]))
                    last = nc.vector.tensor_copy(w4[:, :, g, 0:NE], wb[b][:, g, :, :])
                    if g < 2:
                        link(nc.vector.tensor_tensor(wres[b][:, :, :], wres[b][:, :, :], wb[b][:, g, :, :], ALU.subtract))
                last.then_inc(s("wcat_ready"), 1)
                dve.wait_ge(s("wt_psum"), b + 1)
                nc.vector.tensor_copy(wT[:, b, :], PB(b)[0:3 * NG, 0, :]).then_inc(s("wt_ready"), 1)

            steps = {"ln0": ln0, "qkv": qkv, "gates": gates, "u": u, "scan": scan, "out": out_, "wo": wo,
                     "ln2": ln2, "ln3": ln3, "route": route}
            for name, b in order():
                if name[:2] == "ff":
                    ff(b, int(name[2:]))
                elif name in steps:
                    steps[name](b)

            def moe(b, at):
                dve.wait_ge(s("mu_psum"), at + b + 1)
                dve.wait_ge(s("msilu"), at + b + 1)
                nc.vector.tensor_tensor(W[0][2][:, b, :], W[0][1][:, b, :], PS[2][:, 1, :],
                                        ALU.mult).then_inc(s("mprod"), 1)
                dve.wait_ge(s("mw_psum"), at + b + 1)
                dve.wait_ge(s("mprod"), at + b + 1)
                nc.vector.tensor_tensor(W[0][3][:, b, :], W[0][2][:, b, :], PS[3][:, 0, :],
                                        ALU.mult).then_inc(s("mgated"), 1)
                dve.wait_ge(s("mhi"), at + b + 1)
                nc.vector.tensor_tensor(a_lo[0][:, b, :], W[0][3][:, b, :], f32(a_hi[0][:, b, :]),
                                        ALU.subtract).then_inc(s("mlo"), 1)

            for b in range(NB):
                moe(b, 0)
            with dve.Fori(0, (NM - 1) // 2) as it:
                for j in range(2):
                    for b in range(NB):
                        moe(b, it * 4 + 2 * j + 2)
            for b in range(NB):
                dve.wait_ge(s("mt_psum"), b + 1)
                link(nc.vector.tensor_tensor(tok(W[b][2]), tok(PS[2 + b]), per_token(b, 3), ALU.mult))
                nc.vector.tensor_tensor(hm[b][:, :, :], hm[b][:, :, :], tok(W[b][2]), ALU.add).then_inc(s("y_ready"), 1)

        @block.tensor
        def _(pe):
            mm = nc.tensor.matmul

            def product(out, w_hi, w_lo, r_hi, r_lo, low_ready, start=True, stop=True):
                kk = len(r_hi)
                for m in range(KC):
                    for k in range(kk):
                        mm(out(m), w_hi(k, m), r_hi[k], start=start and k == 0, stop=False)
                        mm(out(m), w_lo(k, m), r_hi[k], start=False, stop=False)
                low_ready()
                for m in range(KC):
                    for k in range(kk):
                        last = mm(out(m), w_hi(k, m), r_lo[k], start=False, stop=stop and k == kk - 1)
                return last

            def small(name, out, b, hi, lo, low_ready):
                return product(lambda m: out[:, m, :], lambda k, m: mat(wsm_hi, name, k, m),
                               lambda k, m: mat(wsm_lo, name, k, m),
                               [hi[:, k, :] for k in range(KC)], [lo[:, k, :] for k in range(KC)], low_ready)

            def head_sum(out, m_, src, start=True, stop=True):
                for c in range(KC):
                    last = mm(out[:, c, :], m_, src[:, c, :], start=start, stop=stop)
                return last

            def to_channels(out, rows):
                for c in range(KC):
                    for t in range(NT):
                        last = nc.tensor.transpose(out[:, c, t * P:(t + 1) * P], rows[:, t, c * P:(c + 1) * P], ident)
                return last

            def to_tokens(out, chans):
                for t in range(NT):
                    for c in range(KC):
                        last = nc.tensor.transpose(out[:, t, c * P:(c + 1) * P], chans[:, c, t * P:(t + 1) * P], ident)
                return last

            cB4 = cB[:, :, :].rearrange("p (k b) m -> p k b m", b=NB)
            pe.wait_ge(s("cB_ready"), 1)
            pe.wait_ge(s("wmod_in"), 48)
            for b in range(NB):
                for k in range(KC):
                    last = mm(PA(b)[:, 0, :], cB4[:, k, b, :], wmod_raw[0][:, k, :], start=k == 0, stop=k == KC - 1)
                last.then_inc(s("mod_shift"), 1)
            for j in range(2 * KC):
                part = wmod_raw[1][:, :, C + j * P:C + (j + 1) * P] if j < KC else \
                    wmod_raw[2][:, :, (j - KC) * P:(j - KC + 1) * P]
                for k in range(KC):
                    last = mm(PB(0)[:, 0, j * NB:(j + 1) * NB], part[:, k, :], cs[:, k * NB:(k + 1) * NB],
                              start=k == 0, stop=k == KC - 1)
            last.then_inc(s("mod_chan"), 1)
            for b in range(NB):
                for g, part in enumerate((wmod_raw[1][:, :, 0:C], wmod_raw[2][:, :, C:2 * C])):
                    for k in range(KC):
                        last = mm(PA(b)[:, 1, g * C:(g + 1) * C], cB4[:, k, b, :], part[:, k, :],
                                  start=k == 0, stop=k == KC - 1)
                last.then_inc(s("mod_gate"), 1)
            pe.wait_ge(s("mats_in"), 16)

            def ln0(b):
                pe.wait_ge(s("hn_ready"), b + 1)
                pe.wait_ge(s("modc_ready"), 1)
                to_channels(PB(b), tok(W[b][1])).then_inc(s("t1_ready"), 1)

            def qkv(b):
                pe.wait_ge(s("h1_full"), b + 1)
                pe.wait_ge(s("mod_used"), b + 1)
                low = lambda: pe.wait_ge(s("h1_lo"), b + 1)
                pe.wait_ge(s("wsm_ready"), 1)
                small("q", PA(b), b, a_hi[b], a_lo[b], low).then_inc(s("q_psum"), 1)
                pe.wait_ge(s("wsm_ready"), 2)
                small("k", PB(b), b, a_hi[b], a_lo[b], low).then_inc(s("k_psum"), 1)
                pe.wait_ge(s("wsm_ready"), 3)
                pe.wait_ge(s("q_used"), b + 1)
                small("v", PA(b), b, a_hi[b], a_lo[b], low).then_inc(s("v_psum"), 1)

            def gates(b):
                pe.wait_ge(s("x_hi"), b + 1)
                pe.wait_ge(s("k_used"), b + 1)
                low = lambda: pe.wait_ge(s("x_lo"), b + 1)
                pe.wait_ge(s("wsm_ready"), 4)
                small("ig", PB(b), b, b_hi[b], b_lo[b], low).then_inc(s("ig_psum"), 1)
                pe.wait_ge(s("wsm_ready"), 5)
                pe.wait_ge(s("v_used"), b + 1)
                small("ga", PA(b), b, b_hi[b], b_lo[b], low).then_inc(s("ga_psum"), 1)
                pe.wait_ge(s("ig_tanh"), b + 1)
                head_sum(PB(b), blk, W[b][5]).then_inc(s("ssk_psum"), 1)
                pe.wait_ge(s("wsm_ready"), 6)
                pe.wait_ge(s("ga_tanh"), b + 1)
                small("og", PA(b), b, b_hi[b], b_lo[b], low).then_inc(s("og_psum"), 1)

            def stat(b):
                pe.wait_ge(s("og_tanh"), b + 1)
                head_sum(PA(b), blk, W[b][6]).then_inc(s("ssv_psum"), 1)

            def u(b):
                pe.wait_ge(s("rk_ready"), b + 1)
                pe.wait_ge(s("u_ready"), b + 1)
                head_sum(PB(b), cen, W[b][3]).then_inc(s("uc_psum"), 1)

            def scan(b):
                pe.wait_ge(s("rv_ready"), b + 1)
                pe.wait_ge(s("sqm_ready"), b + 1)
                head_sum(PA(b), blk, W[b][5]).then_inc(s("ssm_psum"), 1)
                pe.wait_ge(s("mem_ready"), b + 1)
                pe.wait_ge(s("o1_ready"), b + 1)
                head_sum(PB(b), cen, W[b][3]).then_inc(s("oc_psum"), 1)

            def out_(b):
                pe.wait_ge(s("rm_ready"), b + 1)
                pe.wait_ge(s("blk_eps_ready"), 1)
                pe.wait_ge(s("sqo_ready"), b + 1)
                for c in range(KC):
                    mm(PA(b)[:, c, :], blk, W[b][6][:, c, :], start=True, stop=False)
                    last = mm(PA(b)[:, c, :], blk_eps[:, :], W[b][4][:, c, :], start=False, stop=True)
                last.then_inc(s("vo_psum"), 1)

            def wo(b):
                pe.wait_ge(s("wsm_ready"), 7)
                pe.wait_ge(s("ro_ready"), b + 1)
                pe.wait_ge(s("out_hi"), b + 1)
                small("o", PA(b), b, a_hi[b], a_lo[b],
                      lambda: pe.wait_ge(s("out_lo"), b + 1)).then_inc(s("wo_psum"), 1)
                pe.wait_ge(s("gated"), b + 1)
                pe.wait_ge(s("wo_sb"), b + 1)
                to_tokens(tok(PB(b)), W[b][3]).then_inc(s("tw_psum"), 1)

            def ln2(b):
                pe.wait_ge(s("hn2_ready"), b + 1)
                to_channels(PA(b), tok(W[b][1])).then_inc(s("t2_psum"), 1)

            def ff_down(b, f):
                i = b * NF + f
                pe.wait_ge(s("hid_hi"), i + 1)
                pe.wait_ge(s("chunk_split"), 5 + f // 4)
                product(lambda m: PB(b)[:, m, :], lambda k, m: wout_hi[:, f, m * P:(m + 1) * P],
                        lambda k, m: wout_lo[:, f, m * P:(m + 1) * P],
                        [a_hi[b][:, f % 2, :]], [a_lo[b][:, f % 2, :]],
                        lambda: pe.wait_ge(s("hid_lo"), i + 1),
                        start=f == 0, stop=f == NF - 1).then_inc(s("down_done"), 1)

            def half_ff(b, f, which, ready):
                o = (2 * f + which) * P
                out = PA(b)[:, which, :]
                for k in range(KC):
                    mm(out, wff_hi[:, k, o:o + P], b_hi[b][:, k, :], start=k == 0, stop=False)
                    mm(out, wff_lo[:, k, o:o + P], b_hi[b][:, k, :], start=False, stop=False)
                pe.wait_ge(s("h2_lo"), b + 1)
                for k in range(KC):
                    last = mm(out, wff_hi[:, k, o:o + P], b_lo[b][:, k, :], start=False, stop=k == KC - 1)
                last.then_inc(s(ready), 1)

            def ff(b, f):
                i = b * NF + f
                if f == 0:
                    pe.wait_ge(s("h2_full"), b + 1)
                    pe.wait_ge(s("tw_used"), b + 1)
                if f:
                    pe.wait_ge(s("silu_done"), i)
                pe.wait_ge(s("chunk_split"), 1 + f // 2)
                half_ff(b, f, 0, "g_psum")
                if f:
                    pe.wait_ge(s("prod_done"), i)
                half_ff(b, f, 1, "v2_psum")
                if f:
                    ff_down(b, f - 1)

            def acc(b):
                ff_down(b, NF - 1)
                pe.wait_ge(s("acc_sb"), b + 1)
                to_tokens(tok(PA(b)), W[b][3]).then_inc(s("tm_psum"), 1)

            def ln3(b):
                pe.wait_ge(s("hn3_ready"), b + 1)
                to_channels(PB(b), tok(W[b][1])).then_inc(s("t3_psum"), 1)

            def route(b):
                pe.wait_ge(s("wg_in"), 16)
                pe.wait_ge(s("h3_full"), b + 1)
                pe.wait_ge(s("tm_used"), b + 1)
                for t in range(NT):
                    for k in range(KC):
                        last = mm(tok(PA(b))[:, t, 0:NE], W[b][3][:, k, t * P:(t + 1) * P], wg_sb[:, k, :],
                                  start=k == 0, stop=k == KC - 1)
                last.then_inc(s("lg_psum"), 1)
                pe.wait_ge(s("wcat_ready"), b + 1)
                for t in range(NT):
                    last = nc.tensor.transpose(PB(b)[0:3 * NG, 0, t * P:(t + 1) * P], wcat[b][:, t, :], ident)
                last.then_inc(s("wt_psum"), 1)

            steps = {"ln0": ln0, "qkv": qkv, "gates": gates, "stat": stat, "u": u, "scan": scan, "out": out_,
                     "wo": wo, "ln2": ln2, "acc": acc, "ln3": ln3, "route": route}
            for name, b in order():
                if name[:2] == "ff":
                    ff(b, int(name[2:]))
                elif name in steps:
                    steps[name](b)

            gate_bank, up_bank, w_bank = PS[2][:, 0, :], PS[2][:, 1, :], PS[3][:, 0, :]

            def moe_half(j, b, which, bank):
                for k in range(KC):
                    mm(bank, mgu(wsm_hi, j, k, which), b_hi[b][:, k, :], start=k == 0, stop=False)
                    mm(bank, mgu(wsm_lo, j, k, which), b_hi[b][:, k, :], start=False, stop=False)
                    last = mm(bank, mgu(wsm_hi, j, k, which), b_lo[b][:, k, :], start=False, stop=k == KC - 1)
                return last

            def moe_up(j, b, at, i):
                if at is not None:
                    pe.wait_ge(s("msilu"), at)
                moe_half(j, b, 0, gate_bank).then_inc(s("mg_psum"), 1)
                if at is not None:
                    pe.wait_ge(s("mgated"), at)
                moe_half(j, b, 1, up_bank).then_inc(s("mu_psum"), 1)
                mm(w_bank, sel_bf[:, bass.ts(i, P)], wT[:, b, :], start=True, stop=True).then_inc(s("mw_psum"), 1)

            def moe_down(j, b, at, start=False, stop=False):
                pe.wait_ge(s("mhi"), at)
                for m in range(KC):
                    mm(PS[b][:, m, :], mdn(wsm_hi, j, m), a_hi[0][:, b, :], start=start, stop=False)
                    mm(PS[b][:, m, :], mdn(wsm_lo, j, m), a_hi[0][:, b, :], start=False, stop=False)
                pe.wait_ge(s("mlo"), at)
                for m in range(KC):
                    last = mm(PS[b][:, m, :], mdn(wsm_hi, j, m), a_lo[0][:, b, :], start=False, stop=stop)
                last.then_inc(s("mdown"), 1)
                return last

            pe.wait_ge(s("h3_lo"), NB)
            pe.wait_ge(s("wt_ready"), NB)
            pe.wait_ge(s("chunk_split"), len(CH))
            pe.wait_ge(s("moe_ready0"), 1)
            moe_up(0, 0, None, 0)
            pe.wait_ge(s("zeros_ready"), 1)
            for m in range(KC):
                mm(PS[1][:, m, :], zeros[:, 0:P], zeros[:, :], start=True, stop=False)
            moe_up(0, 1, 1, 0)
            moe_down(0, 0, 1, start=True)
            with pe.Fori(0, (NM - 1) // 2) as it:
                for jj in range(2):
                    j = 1 - jj
                    base = it * 4 + 2 * jj + 2
                    if j == 1:
                        pe.wait_ge(s("moe_ready1"), it + 1)
                    else:
                        pe.wait_ge(s("moe_ready0"), it + 2)
                    moe_up(j, 0, base, it * 2 + jj + 1)
                    moe_down(1 - j, 1, base)
                    moe_up(j, 1, base + 1, it * 2 + jj + 1)
                    moe_down(j, 0, base + 1)
            for m in range(KC):
                last = mm(PS[0][:, m, :], zeros[:, 0:P], zeros[:, :], start=False, stop=True)
            last.then_inc(s("mdown"), 1)
            moe_down(0, 1, 2 * NM, stop=True)
            for b in range(NB):
                pe.wait_ge(s("macc_sb"), b + 1)
                to_tokens(tok(PS[2 + b]), W[b][0]).then_inc(s("mt_psum"), 1)


def kernel(**inputs):
    import numpy as np
    import concourse.bacc as bacc
    from concourse.bass_utils import run_bass_kernel_spmd

    a = {k.replace("L0_", ""): np.asarray(v) for k, v in inputs.items()}
    f = np.float32

    def rows(w):
        return np.ascontiguousarray(w.reshape(-1, P, w.shape[1]).transpose(1, 0, 2))

    per_channel = {
        "ln1w": a["attn_ln1w"], "ln1b": a["attn_ln1b"], "cb": a["attn_conv_b"], "big": a["attn_big"],
        "bg": np.repeat(a["attn_bg"], HD), "bog": a["attn_bog"], "gnw": a["attn_gnw"], "gnb": a["attn_gnb"],
        "ln2w": a["attn_ln2w"], "ln2b": a["attn_ln2b"],
        **{f"cw{k}": a["attn_conv_w"][:, 0, k] for k in range(KCONV)},
    }
    par = np.concatenate([per_channel[n].reshape(KC, P).T for n in COLS]
                         + [np.tile(a["attn_" + n], P // HD)[:, None] for n in ONCE], axis=1)
    wsm = rows(np.concatenate([a["attn_Wq"], a["attn_Wk"], a["attn_Wv"], a["attn_Wig"],
                               np.repeat(a["attn_Wg"], HD, axis=1), a["attn_Wog"], a["attn_Wo"]], axis=1))
    gv = np.stack([a["attn_Wgate"].reshape(C, NF, P), a["attn_Wval"].reshape(C, NF, P)], axis=2)
    wff = rows(gv.reshape(C, 2 * FF))
    wout = rows(a["attn_Wout"])
    gu, sg = a["ffn_gate_up_weights"], a["ffn_shared_gate_up"]
    fill = NM * P - HIDDEN
    gate = np.concatenate([gu[:, :FE].reshape(-1, C), sg[:2 * FE], np.zeros((fill, C), f)])
    up = np.concatenate([gu[:, FE:].reshape(-1, C), sg[2 * FE:], np.zeros((fill, C), f)])
    down = np.concatenate([a["ffn_down_weights"].transpose(0, 2, 1).reshape(-1, C), a["ffn_shared_down"].T,
                           np.zeros((fill, C), f)])
    g = np.stack([gate, up]).reshape(2, NM, P, KC, P).transpose(1, 4, 3, 0, 2).reshape(NM, P, 2 * KC * P)
    wmoe = np.concatenate([g, down.reshape(NM, P, C)], axis=2)
    unit = np.minimum(np.arange(NM * P) // FE, NE)
    sel = np.tile((unit[None, :] == np.arange(NG)[:, None]).astype(f), (3, 1))
    head = np.arange(P) // HD
    block_mean = ((head[:, None] == head[None, :]) / HD).astype(f)
    mats = np.stack([np.eye(P, dtype=f), block_mean, np.eye(P, dtype=f) - block_mean], axis=1)

    arrays = {
        "x": a["attn_x"].reshape(NB * T, C),
        "cT": a["c"].T.reshape(KC, P, NB).transpose(1, 0, 2).reshape(P, KC * NB),
        "wmod": rows(a["wmod"]), "par": par, "wsm": wsm, "wff": wff, "wout": wout,
        "wgate": rows(np.ascontiguousarray(a["ffn_gate_weight"].T)), "wmoe": wmoe, "sel": sel, "mats": mats,
    }
    arrays = {"in_" + k: np.ascontiguousarray(v) for k, v in arrays.items()}
    nc = bacc.Bacc("TRN2", target_bir_lowering=False, num_devices=1, dynamic_dma_scratch_size=1024)
    args = [nc.dram_tensor(k, v.shape, FP32, kind="ExternalInput").ap() for k, v in arrays.items()]
    args.append(nc.dram_tensor("out", (NB * T, C), FP32, kind="ExternalOutput").ap())
    adaln_block_kernel(nc, *args)
    r = run_bass_kernel_spmd(nc, [arrays], core_ids=[0])
    return np.asarray(r.results[0]["out"]).reshape(NB, T, C)
```

```python
import concourse.bass as bass
from concourse import mybir
from contextlib import ExitStack

FP32 = mybir.dt.float32
FP32R = mybir.dt.float32r
BF16 = mybir.dt.bfloat16
ALU = mybir.AluOpType
ACT = mybir.ActivationFunctionType
AX = mybir.AxisListType

P = 128
NB = 2
T = 512
C = 256
KC = C // P
NT = T // P
NH, HD = 16, 16
KCONV = 4
PAD = KCONV - 1
FF = 1024
NF = FF // P
NE, FE = 16, 176
NG = NE + 1
HIDDEN = NE * FE + 2 * FE
NM = -(-HIDDEN // P)
WM = 2 * KC * P + C
TOPK = 4
EPS = 1e-5
LN_HALF = -0.6931471805599453

COLS = ["ln1w", "ln1b", "cw0", "cw1", "cw2", "cw3", "cb", "big", "bg", "bog", "gnw", "gnb", "ln2w", "ln2b"]
ONCE = ["vnw", "vnb", "mnw", "mnb"]
NPAR = 2 * len(COLS) + len(ONCE)
MATS = ["q", "k", "ig", "v", "ga", "og", "o"]

LOG_SET, SILU_SET = "natural_log_exp_and_others", "silu_and_others"

LEAD = 8
NQ = NM + LEAD
SLOTS = 4
NCH_FF, NCH_OUT, NCH_SEL = 4, 2, -(-NM // 8)


TENSOR_PLAN = """
    shift.0 shift.1 modulation.0 modulation.1 t1.0 q.0 t1.1 k.0 q.1 k.1 v.0 ig.0 ga.0 ssk.0 og.0 v.1 ssv.0 ig.1
    ga.1 u.0 ssk.1 mem.0 og.1 oc.0 vo.0 ssv.1 wo.0 tw.0 u.1 mem.1 oc.1 t2.0 vo.1 up.0.0 wo.1 up.0.1 tw.1
    down.0.0 up.0.2 down.0.1 up.0.3 down.0.2 up.0.4 down.0.3 t2.1 up.0.5 down.0.4 up.0.6 down.0.5 up.0.7
    down.0.6 down.0.7 up.1.0 tm.0 up.1.1 down.1.0 up.1.2 down.1.1 up.1.3 down.1.2 up.1.4 t3.0 down.1.3 up.1.5
    logits.0 down.1.4 up.1.6 down.1.5 up.1.7 wt.0 down.1.6 down.1.7 tm.1 eup.0.0 eup.0.1 edown.0.0 eup.0.2
    edown.0.1 eup.0.3 edown.0.2 t3.1 eup.0.4 edown.0.3 eup.0.5 logits.1 edown.0.4 eup.0.6 edown.0.5 wt.1 eup.0.7
    edown.0.6
"""

SCALAR_PLAN = """
    shift.0 shift.1 wsm.0 wsm.1 gate.0 wsm.2 chunk.0 chunk.1 gate.1 h1.0 q.0 h1.1 wsm.3 wsm.4 wsm.5 wsm.6 k.0
    xconv.0 v.0 q.1 k.1 ig.0 ga.0 xconv.1 og.0 rk.0 v.1 rv.0 ig.1 ga.1 sqm.0 rm.0 og.1 sqo.0 ro.0 rk.1 gated.0
    rv.1 wo.0 chunk.2 sqm.1 rm.1 chunk.3 sqo.1 chunk.4 h2.0 ro.1 gated.1 silu.0.0 chunk.5 wo.1 hid.0.0 silu.0.1
    hid.0.1 silu.0.2 hid.0.2 silu.0.3 hid.0.3 silu.0.4 hid.0.4 silu.0.5 hid.0.5 h2.1 silu.0.6 hid.0.6 silu.0.7
    hid.0.7 acc.0 silu.1.0 hid.1.0 silu.1.1 hid.1.1 silu.1.2 hid.1.2 silu.1.3 hid.1.3 silu.1.4 hid.1.4 h3.0
    silu.1.5 hid.1.5 exp.0 ehigh.0.0 silu.1.6 hid.1.6 silu.1.7 ehigh.0.1 hid.1.7 acc.1 ehigh.0.2 esilu.0.0
    ehid.0.0 ehigh.0.3 esilu.0.1 ehid.0.1 ehigh.0.4 esilu.0.2 ehid.0.2 ehigh.0.5 esilu.0.3 ehid.0.3 ehigh.0.6
    esilu.0.4 h3.1 ehid.0.4 ehigh.0.7 esilu.0.5 exp.1 ehid.0.5 ehigh.0.8 esilu.0.6 ehid.0.6 ehigh.0.9 esilu.0.7
    ehid.0.7
"""

VECTOR_PLAN = """
    var0.0 var0.1 scaled0.0 shifted.0 var1.0 scaled0.1 shifted.1 var1.1 hn1.0 vsum scaled modc hn1.1 h1lo.0
    modg.0 modg.1 h1lo.1 conv.0.0 conv.0.1 xlo.0 conv.1.0 conv.1.1 a1.0 xlo.1 gamma.0 uk.0 uv.0 mem.0 a1.1
    gamma.1 o1.0 osig.0 gated.0 uk.1 outlo.0 uv.1 wo.0 mem.1 var2.0 o1.1 osig.1 hn2.0 h2lo.0 gated.1 outlo.1
    prod.0.0 hidlo.0.0 prod.0.1 wo.1 var2.1 hidlo.0.1 prod.0.2 hidlo.0.2 prod.0.3 hidlo.0.3 hn2.1 prod.0.4
    hidlo.0.4 prod.0.5 hidlo.0.5 prod.0.6 hidlo.0.6 prod.0.7 hidlo.0.7 h2lo.1 prod.1.0 hidlo.1.0 sum3.0 gated3.0
    prod.1.1 plus_x.0 hidlo.1.1 var3.0 prod.1.2 hidlo.1.2 prod.1.3 hn3.0 hidlo.1.3 prod.1.4 hidlo.1.4 h3lo.0
    prod.1.5 lgsub.0 hidlo.1.5 topk.0 prod.1.6 hidlo.1.6 prod.1.7 hidlo.1.7 wt.0 sum3.1 gated3.1 egated.0.0
    plus_x.1 elo.0.0 var3.1 egated.0.1 elo.0.1 egated.0.2 elo.0.2 hn3.1 egated.0.3 elo.0.3 egated.0.4 h3lo.1
    elo.0.4 egated.0.5 lgsub.1 topk.1 elo.0.5 egated.0.6 elo.0.6 egated.0.7 elo.0.7 wt.1
"""

POOL_PLAN = """
    rstd.0.0 rstd.1.0 wsm.0 rstd.0.1 rstd.1.1 wsm.1 vcentre wsm.2 wsm.3 wsm.4 sqk.0 wsm.5 sqv.0 wsm.6 sqk.1
    chunk.0 chunk.1 sqq.0 sqq.1 sqv.1 chunk.2 rstd.0.2 chunk.3 chunk.4 chunk.5 chunk.6 rstd.1.2 chunk.7 chunk.8
    chunk.9 rstd.0.3 elow.0 elow.1 elow.2 elow.3 rstd.1.3 elow.4 elow.5 elow.6 elow.7
"""


def plan(text):
    for step in text.split():
        name, *args = step.split(".")
        yield name, [int(a) for a in args]


def adaln_block_kernel(nc, x, cT, wmod, par, wsm, wff, wout, wgate, wmoe, sel, mats, out):
    ctx = ExitStack()
    with ctx:
        def sb(name, shape, dt=FP32):
            return ctx.enter_context(nc.sbuf_tensor(name, shape, dt))

        def sem(name):
            return ctx.enter_context(nc.semaphore(name))

        mats_sb = sb("mats_sb", [P, 3, P])
        ident, blk, cen = (mats_sb[:, i, :] for i in range(3))
        blk_eps = sb("blk_eps", [P, P])
        par_sb = sb("par_sb", [P, NPAR])
        half = sb("half", [P, NPAR])
        wg_sb = sb("wg_sb", [P, KC, NE])
        cT_sb = sb("cT_sb", [P, KC * NB])
        cs = sb("cs", [P, KC * NB])
        cB = sb("cB", [P, KC * NB, P])
        const = sb("const", [P, 6])
        mod = sb("mod", [P, NB, 4, C])
        modc = sb("modc", [P, 2 * KC, NB])
        gtmp = sb("gtmp", [P, 2, C])

        wsm_hi = sb("wsm_hi", [P, KC, len(MATS) * C], FP32R)
        wsm_lo = sb("wsm_lo", [P, KC, len(MATS) * C], FP32R)
        wff_hi = sb("wff_hi", [P, KC, 2 * FF], FP32R)
        wff_lo = sb("wff_lo", [P, KC, 2 * FF], FP32R)
        wout_hi = sb("wout_hi", [P, NF, C], FP32R)
        wout_lo = sb("wout_lo", [P, NF, C], FP32R)
        stage = sb("stage", [P, 2, 1024])
        sel_bf = sb("sel_bf", [3 * NG, NM * P], BF16)
        zeros = sb("zeros", [P, T], BF16)
        vmean = sb("vmean", [P, KC * NH])

        hm = [sb(f"hm{b}", [P, NT, C]) for b in range(NB)]
        hpad = [sb(f"hpad{b}", [P, KC, PAD + T]) for b in range(NB)]
        W = [[sb(f"w{b}_{i}", [P, KC, T]) for i in range(7)] for b in range(NB)]
        a_hi = [sb(f"a_hi{b}", [P, KC, T], FP32R) for b in range(NB)]
        a_lo = [sb(f"a_lo{b}", [P, KC, T], FP32R) for b in range(NB)]
        b_hi = [sb(f"b_hi{b}", [P, KC, T], FP32R) for b in range(NB)]
        b_lo = [sb(f"b_lo{b}", [P, KC, T], FP32R) for b in range(NB)]
        st = [sb(f"st{b}", [P, NT, 6]) for b in range(NB)]
        mv = [sb(f"mv{b}", [P, NT, 2]) for b in range(NB)]
        rr = [sb(f"rr{b}", [P, NT]) for b in range(NB)]
        top8 = [sb(f"top8{b}", [P, NT, 8]) for b in range(NB)]
        sc = [sb(f"sc{b}", [P, NT, NE + 4]) for b in range(NB)]
        rep = [sb(f"rep{b}", [P, NT, NE + 4]) for b in range(NB)]
        sums = [sb(f"sums{b}", [P, NT]) for b in range(NB)]
        wres = [sb(f"wres{b}", [P, NT, NE]) for b in range(NB)]
        wb = [sb(f"wb{b}", [P, 3, NT, NE], BF16) for b in range(NB)]
        wcat = [sb(f"wcat{b}", [P, NT, 3 * NG]) for b in range(NB)]
        wT = sb("wT", [3 * NG, NB, T], BF16)

        PS = [ctx.enter_context(nc.psum_tensor(f"ps{i}", [P, 2, T], FP32)) for i in range(4)]
        PA = lambda b: PS[2 * b]
        PB = lambda b: PS[2 * b + 1]
        tok = lambda ps: ps[:, :, :].rearrange("p a (t c) -> p (a t) c", c=C)

        wmod_raw = [W[0][2 + i] for i in range(3)]
        wsm_raw = [W[1][3 + i] for i in range(4)]

        v_raw = wsm_raw[MATS.index("v") // 2][:, :, MATS.index("v") % 2 * C:(MATS.index("v") % 2 + 1) * C]

        def col(name, c=0, of=None):
            j = 2 * COLS.index(name) + c if name in COLS else 2 * len(COLS) + ONCE.index(name)
            return (par_sb if of is None else of)[:, j:j + 1]

        def mat(w, name, k, m):
            o = MATS.index(name) * C + m * P
            return w[:, k, o:o + P]

        f32 = lambda ap: ap.bitcast(FP32)

        S = {}

        def s(name):
            return S[name]

        for name in (
            "cT_in par_in mats_in wg_in x_again out_done "
            "cs_ready cB_ready const_ready zeros_ready par_half blk_eps_ready "
            "mod_shift mod_shift_sb mod_gate mod_gate_sb mod_chan modc_ready modg_ready "
            "wsm_hi_ready vsum_ready vcentred wsm_ready chunk_hi chunk_split "
            "var0 rstd0 var1 rstd1 hn_ready t1_psum h1_full h1_lo "
            "q_psum q_used sqq_ready sqk_ready sqv_ready k_psum k_used v_psum v_used conv_ready x_hi x_lo "
            "ig_psum ig_tanh ga_psum ga_tanh og_psum og_tanh a1_done gamma_ready "
            "ssk_psum rk_ready ssv_psum rv_ready u_ready uc_psum mem_ready "
            "sqm_ready ssm_psum rm_ready o1_ready oc_psum sqo_ready vo_psum ro_ready "
            "gated out_hi out_lo wo_psum wo_sb tw_psum tw_used var2 rstd2 hn2_ready t2_psum h2_full h2_lo "
            "g_psum v2_psum silu_done prod_done hid_hi hid_lo down_done acc_sb tm_psum tm_used "
            "var3 rstd3 hn3_ready t3_psum h3_full h3_lo lg_psum lg_sub exp_done wcat_ready wt_psum wt_ready "
            "dve_order act_order pool_order moe_hi moe_ready msum_sb mt_psum y_ready"
        ).split():
            S[name] = sem(name)
        x_in = [sem(f"x_in{b}") for b in range(NB)]
        wmod_in = [sem(f"wmod_in{i}") for i in range(3)]
        for name in "mg_psum mu_psum mw_psum msilu mprod mgated mhi mlo mdown".split():
            for b in range(NB):
                S[f"{name}{b}"] = sem(f"{name}{b}")
        stage_in = [sem(f"stage_in{i}") for i in range(2)]
        wsm_in = [sem(f"wsm_in{i}") for i in range(4)]
        raw_in = [sem(f"raw_in{i}") for i in range(2)]

        CH = [("ff", i) for i in range(NCH_FF)] + [("out", i) for i in range(NCH_OUT)] + [("sel", i) for i in range(NCH_SEL)]

        def chunk(c):
            kind, i = CH[c]
            slot = stage[:, c % 2, :]
            if kind == "ff":
                return (slot.rearrange("p (k n) -> p k n", k=KC), wff_hi[:, :, i * 512:(i + 1) * 512],
                        wff_lo[:, :, i * 512:(i + 1) * 512])
            if kind == "out":
                return (slot.rearrange("p (f n) -> p f n", n=C), wout_hi[:, 4 * i:4 * i + 4, :],
                        wout_lo[:, 4 * i:4 * i + 4, :])
            w = min(1024, NM * P - i * 1024)
            return slot[0:3 * NG, 0:w], sel_bf[:, i * 1024:i * 1024 + w], None

        def raw_slot(j):
            return W[1][4 + j][:, :, :].rearrange("p a n -> p (a n)")[:, 0:WM]

        flat = {id(w): w[:, :, :].rearrange("p k n -> p (k n)") for w in (wsm_hi, wsm_lo)}

        def mw(w, j, o=0, n=WM):
            return flat[id(w)][:, j * WM + o:j * WM + o + n]

        def mgu(w, j, k, which):
            return mw(w, j, (2 * k + which) * P, P)

        def mdn(w, j, m):
            return mw(w, j, 2 * KC * P + m * P, P)

        block = ctx.enter_context(nc.Block())

        @block.sync
        def _(sp):
            def load_wsm(i):
                n = min(2 * C, len(MATS) * C - i * 2 * C)
                sp.dma_start(wsm_raw[i][:, :, 0:n], wsm[:, :, i * 2 * C:i * 2 * C + n]).then_inc(wsm_in[i], 16)

            def load_x(b, ready):
                sp.dma_start(tok(W[b][0]), x[b * T:(b + 1) * T, :].rearrange("(t p) c -> p t c", p=P)).then_inc(ready, 16)

            def load_wmod(i):
                sp.dma_start(wmod_raw[i][:, :, :], wmod[:, :, i * T:(i + 1) * T]).then_inc(wmod_in[i], 16)

            sp.dma_start(cT_sb[:, :], cT).then_inc(s("cT_in"), 16)
            load_x(0, x_in[0])
            load_wmod(0)
            sp.dma_start(mats_sb[:, :, :], mats).then_inc(s("mats_in"), 16)
            sp.dma_start(par_sb[:, :], par).then_inc(s("par_in"), 16)
            load_x(1, x_in[1])
            load_wmod(1)
            load_wmod(2)
            load_wsm(0)
            load_wsm(1)
            load_wsm(2)
            load_wsm(3)
            sp.dma_start(wg_sb[:, :, :], wgate).then_inc(s("wg_in"), 16)
            for n, (kind, i) in enumerate(CH):
                if n >= 2:
                    sp.wait_ge(s("chunk_split"), n - 1)
                src = {"ff": lambda: wff[:, :, i * 512:(i + 1) * 512], "out": lambda: wout[:, 4 * i:4 * i + 4, :],
                       "sel": lambda: sel[:, i * 1024:min((i + 1) * 1024, NM * P)]}[kind]()
                sp.dma_start(chunk(n)[0], src).then_inc(stage_in[n % 2], 16)
            for b in range(NB):
                sp.wait_ge(s("gated"), KC * (b + 1))
                if b:
                    sp.wait_ge(s("x_again"), 16)
                load_x(b, s("x_again"))
            sp.wait_ge(s("vo_psum"), KC * NB)
            sp.wait_ge(s("o1_ready"), KC * NB)
            for q in range(2):
                sp.dma_start(raw_slot(q), wmoe[q, :, :]).then_inc(raw_in[q], 16)
            with sp.Fori(1, NM // 2) as it:
                for j in range(2):
                    sp.wait_ge(s("moe_ready"), it * 2 + j - 1)
                    sp.dma_start(raw_slot(j), wmoe[it * 2 + j, :, :]).then_inc(raw_in[j], 16)
            for q in range(NM // 2 * 2, NQ):
                sp.wait_ge(s("moe_ready"), q - 1)
                sp.dma_start(raw_slot(q % 2), wmoe[q % NM, :, :]).then_inc(raw_in[q % 2], 16)
            for b in range(NB):
                sp.wait_ge(s("y_ready"), b + 1)
                sp.dma_start(out[b * T:(b + 1) * T, :].rearrange("(t p) c -> p t c", p=P),
                             hm[b][:, :, :]).then_inc(s("out_done"), 16)
            sp.wait_ge(s("out_done"), 16 * NB)

        @block.gpsimd
        def _(pool):
            n = [0]

            def link(ins):
                ins.then_inc(s("pool_order"), 1)
                n[0] += 1
                pool.wait_ge(s("pool_order"), n[0])

            def low(lo, raw, hi):
                return nc.gpsimd.tensor_tensor(lo, raw, f32(hi), ALU.subtract)

            for i, v in enumerate((EPS, 1e-12, EPS * 1e-12, LN_HALF, 1.0, -0.5)):
                nc.gpsimd.memset(const[:, i:i + 1], v)
            for b in range(NB):
                w4 = wcat[b][:, :, :].rearrange("p t (g e) -> p t g e", e=NG)
                nc.gpsimd.memset(w4[:, :, 1:3, NE:NG], 0.0)
                nc.gpsimd.memset(w4[:, :, 0, NE:NG], 1.0)
                for i in range(4):
                    nc.gpsimd.memset(sc[b][:, :, NE + i:NE + i + 1], -5.0 - i)
                last = nc.gpsimd.memset(hpad[b][:, :, 0:PAD], 0.0)
            last.then_inc(s("const_ready"), 1)
            nc.gpsimd.memset(zeros[:, :], 0.0).then_inc(s("zeros_ready"), 1)

            def wsm_low(m):
                raw = wsm_raw[m // 2][:, :, (m % 2) * C:(m % 2 + 1) * C]
                pool.wait_ge(s("wsm_hi_ready"), m + 1)
                low(wsm_lo[:, :, m * C:(m + 1) * C], raw, wsm_hi[:, :, m * C:(m + 1) * C]).then_inc(s("wsm_ready"), 1)

            def centre_v():
                pool.wait_ge(s("vsum_ready"), 1)
                g = v_raw.rearrange("p k (h d) -> p k h d", d=HD)
                vm = vmean[:, :].rearrange("p (k h) -> p k h", k=KC)
                for k in range(KC):
                    last = nc.gpsimd.tensor_tensor(g[:, k], g[:, k],
                                                   vm[:, k].unsqueeze(2).broadcast_to([P, NH, HD]), ALU.subtract)
                last.then_inc(s("vcentred"), 1)

            def square(b, dst, src, given, ready):
                if b == 0:
                    pool.wait_ge(s("mod_chan"), 1)
                    pool.wait_ge(s("mod_gate"), NB)
                else:
                    pool.wait_ge(s("wsm_ready"), len(MATS))
                for c in range(KC):
                    pool.wait_ge(s(given), KC * b + c + 1)
                    nc.gpsimd.tensor_tensor(W[b][dst][:, c, :], W[b][src][:, c, :], W[b][src][:, c, :],
                                            ALU.mult).then_inc(s(ready), 1)

            def chunk_low(c):
                kind, i = CH[c]
                raw, hi, lo = chunk(c)
                if kind == "sel":
                    pool.wait_ge(stage_in[c % 2], 16 * (c // 2 + 1))
                    ins = nc.gpsimd.tensor_copy(hi, raw)
                else:
                    pool.wait_ge(s("chunk_hi"), c + 1)
                    ins = low(lo, raw, hi)
                ins.then_inc(s("chunk_split"), 1)

            def rstd(b, i):
                pool.wait_ge(s(f"var{i}"), b + 1)
                link(nc.gpsimd.tensor_scalar(rr[b][:, :], mv[b][:, :, 1], EPS, None, ALU.add))
                nc.gpsimd.tensor_tensor(rr[b][:, :], rr[b][:, :], const[:, 5:6].broadcast_to([P, NT]),
                                        ALU.pow).then_inc(s(f"rstd{i}"), 1)

            def moe_low(q):
                low(mw(wsm_lo, q % SLOTS), raw_slot(q % 2), mw(wsm_hi, q % SLOTS)).then_inc(s("moe_ready"), 1)

            def moe_low_first(q):
                pool.wait_ge(s("moe_hi"), q + 1)
                moe_low(q)

            steps = {
                "sqq": lambda b: square(b, 4, 1, "q_used", "sqq_ready"),
                "sqk": lambda b: square(b, 5, 2, "k_used", "sqk_ready"),
                "sqv": lambda b: square(b, 6, 3, "v_used", "sqv_ready"),
                "wsm": wsm_low, "vcentre": centre_v, "chunk": chunk_low, "rstd": rstd, "elow": moe_low_first,
            }
            for name, args in plan(POOL_PLAN):
                steps[name](*args)

            with pool.Fori(LEAD // SLOTS, NQ // SLOTS) as it:
                for j in range(SLOTS):
                    pool.wait_ge(s("moe_hi"), it * SLOTS + j + 1)
                    moe_low(j)
            for q in range(NQ // SLOTS * SLOTS, NQ):
                moe_low_first(q)

        @block.scalar
        def _(act):
            n = [0]
            loaded = [None]

            def link(ins):
                ins.then_inc(s("act_order"), 1)
                n[0] += 1
                act.wait_ge(s("act_order"), n[0])

            def table(name):
                if loaded[0] != name:
                    nc.scalar.preload_act_table_set(name)
                    loaded[0] = name

            eps, tiny, epstiny, lnhalf, one = (const[:, i:i + 1] for i in range(5))

            def rsqrt(out, in_, bias, scale=1.0, bias2=0.0):
                table(LOG_SET)
                link(nc.scalar.activation(out, in_, ACT.Ln, bias=bias, scale=scale))
                return nc.scalar.activation(out, out, ACT.Exp, scale=-0.5, bias=bias2)

            table(SILU_SET)
            act.wait_ge(s("cT_in"), 16)
            nc.scalar.activation(cs[:, :], cT_sb[:, :], ACT.Silu).then_inc(s("cs_ready"), 1)
            act.wait_ge(s("const_ready"), 1)

            def to_high_and_full(b, hi, full, ps, scale, bias, ready):
                for c in range(KC):
                    nc.scalar.activation(full(c), ps[:, c, :], ACT.Identity, scale=scale(c), bias=bias(c))
                    nc.scalar.activation(hi[:, c, :], ps[:, c, :], ACT.Identity, scale=scale(c),
                                         bias=bias(c)).then_inc(s(ready), 1)

            def wsm_high(m):
                if MATS[m] == "v":
                    act.wait_ge(s("vcentred"), 1)
                else:
                    act.wait_ge(wsm_in[m // 2], 16)
                nc.scalar.activation(wsm_hi[:, :, m * C:(m + 1) * C],
                                     wsm_raw[m // 2][:, :, (m % 2) * C:(m % 2 + 1) * C],
                                     ACT.Copy).then_inc(s("wsm_hi_ready"), 1)

            def shift(b):
                act.wait_ge(s("mod_shift"), b + 1)
                nc.scalar.activation(mod[:, b, 1, :], PA(b)[:, 0, C:2 * C], ACT.Identity, bias=one)
                nc.scalar.activation(mod[:, b, 0, :], PA(b)[:, 0, 0:C], ACT.Copy).then_inc(s("mod_shift_sb"), 1)

            def h1(b):
                act.wait_ge(s("par_in"), 16)
                act.wait_ge(s("t1_psum"), b + 1)
                to_high_and_full(b, a_hi[b], lambda c: hpad[b][:, c, PAD:PAD + T], PB(b),
                                 lambda c: col("ln1w", c), lambda c: col("ln1b", c), "h1_full")

            def gate(b):
                act.wait_ge(s("mod_gate"), b + 1)
                nc.scalar.activation(mod[:, b, 2:4, :], PA(b)[:, 1, :].rearrange("p (j c) -> p j c", c=C),
                                     ACT.Copy).then_inc(s("mod_gate_sb"), 1)

            def q(b):
                for m in range(KC):
                    act.wait_ge(s("q_psum"), KC * b + m + 1)
                    nc.scalar.activation(W[b][1][:, m, :], PA(b)[:, m, :], ACT.Copy).then_inc(s("q_used"), 1)

            def k(b):
                if b == 0:
                    act.wait_ge(s("mod_gate"), NB)
                for m in range(KC):
                    act.wait_ge(s("k_psum"), KC * b + m + 1)
                    nc.scalar.activation(W[b][2][:, m, :], PB(b)[:, m, :], ACT.Copy).then_inc(s("k_used"), 1)

            def xconv(b):
                table(SILU_SET)
                for c in range(KC):
                    act.wait_ge(s("conv_ready"), KC * b + c + 1)
                    link(nc.scalar.activation(W[b][0][:, c, :], W[b][0][:, c, :], ACT.Silu))
                    nc.scalar.activation(b_hi[b][:, c, :], W[b][0][:, c, :], ACT.Copy).then_inc(s("x_hi"), 1)

            def v(b):
                if b:
                    act.wait_ge(s("wsm_ready"), len(MATS))
                else:
                    act.wait_ge(s("mod_chan"), 1)
                for m in range(KC):
                    act.wait_ge(s("v_psum"), KC * b + m + 1)
                    nc.scalar.activation(W[b][3][:, m, :], PA(b)[:, m, :], ACT.Copy).then_inc(s("v_used"), 1)

            def tanh_half(b, dst, ps, bias, given, ready):
                table(SILU_SET)
                for c in range(KC):
                    act.wait_ge(s(given), KC * b + c + 1)
                    nc.scalar.activation(dst[:, c, :], ps[:, c, :], ACT.Tanh, scale=0.5,
                                         bias=col(bias, c, of=half)).then_inc(s(ready), 1)

            def ig(b):
                act.wait_ge(s("par_half"), 1)
                act.wait_ge(s("x_lo"), KC * (b + 1))
                tanh_half(b, W[b][0], PB(b), "big", "ig_psum", "ig_tanh")

            def ga(b):
                tanh_half(b, hpad[b][:, :, 0:T], PA(b), "bg", "ga_psum", "ga_tanh")

            def og(b):
                act.wait_ge(s("a1_done"), KC * (b + 1))
                tanh_half(b, W[b][0], PA(b), "bog", "og_psum", "og_tanh")

            def rk(b):
                table(LOG_SET)
                for c in range(KC):
                    act.wait_ge(s("ssk_psum"), KC * b + c + 1)
                    rsqrt(W[b][5][:, c, :], PB(b)[:, c, :], tiny, scale=float(HD),
                          bias2=lnhalf).then_inc(s("rk_ready"), 1)

            def rv(b):
                table(LOG_SET)
                for c in range(KC):
                    act.wait_ge(s("ssv_psum"), KC * b + c + 1)
                    rsqrt(W[b][6][:, c, :], PA(b)[:, c, :], eps).then_inc(s("rv_ready"), 1)

            def sqm(b):
                for c in range(KC):
                    act.wait_ge(s("mem_ready"), KC * b + c + 1)
                    nc.scalar.activation(W[b][5][:, c, :], W[b][3][:, c, :], ACT.Square).then_inc(s("sqm_ready"), 1)

            def rm(b):
                table(LOG_SET)
                for c in range(KC):
                    act.wait_ge(s("ssm_psum"), KC * b + c + 1)
                    rsqrt(W[b][5][:, c, :], PA(b)[:, c, :], eps).then_inc(s("rm_ready"), 1)

            def sqo(b):
                for c in range(KC):
                    act.wait_ge(s("oc_psum"), KC * b + c + 1)
                    nc.scalar.activation(W[b][6][:, c, :], PB(b)[:, c, :], ACT.Square).then_inc(s("sqo_ready"), 1)

            def ro(b):
                table(LOG_SET)
                for c in range(KC):
                    act.wait_ge(s("vo_psum"), KC * b + c + 1)
                    rsqrt(W[b][6][:, c, :], PA(b)[:, c, :], epstiny).then_inc(s("ro_ready"), 1)

            def gated(b):
                for c in range(KC):
                    act.wait_ge(s("gated"), KC * b + c + 1)
                    nc.scalar.activation(a_hi[b][:, c, :], W[b][2][:, c, :], ACT.Copy).then_inc(s("out_hi"), 1)

            def wo(b):
                for c in range(KC):
                    act.wait_ge(s("wo_psum"), KC * b + c + 1)
                    nc.scalar.activation(W[b][3][:, c, :], PA(b)[:, c, :], ACT.Copy).then_inc(s("wo_sb"), 1)

            def h2(b):
                act.wait_ge(s("t2_psum"), b + 1)
                to_high_and_full(b, b_hi[b], lambda c: W[b][3][:, c, :], PA(b),
                                 lambda c: col("ln2w", c), lambda c: col("ln2b", c), "h2_full")

            def silu(b, f):
                i = b * NF + f
                table(SILU_SET)
                act.wait_ge(s("g_psum"), i + 1)
                nc.scalar.activation(W[b][1][:, f % 2, :], PA(b)[:, 0, :], ACT.Silu).then_inc(s("silu_done"), 1)

            def hid(b, f):
                i = b * NF + f
                act.wait_ge(s("prod_done"), i + 1)
                if f >= 2:
                    act.wait_ge(s("down_done"), i - 1)
                nc.scalar.activation(a_hi[b][:, f % 2, :], W[b][2][:, f % 2, :], ACT.Copy).then_inc(s("hid_hi"), 1)

            def acc(b):
                act.wait_ge(s("h2_lo"), KC * (b + 1))
                act.wait_ge(s("down_done"), (b + 1) * NF)
                for c in range(KC):
                    nc.scalar.activation(W[b][3][:, c, :], PB(b)[:, c, :], ACT.Copy).then_inc(s("acc_sb"), 1)

            def h3(b):
                act.wait_ge(s("modc_ready"), 1)
                act.wait_ge(s("t3_psum"), b + 1)
                to_high_and_full(b, b_hi[b], lambda c: W[b][3][:, c, :], PB(b),
                                 lambda c: modc[:, KC + c, b:b + 1], lambda c: modc[:, c, b:b + 1], "h3_full")

            def exp(b):
                table(LOG_SET)
                act.wait_ge(s("lg_sub"), b + 1)
                nc.scalar.activation(rep[b][:, :, 0:NE], rep[b][:, :, 0:NE], ACT.Exp).then_inc(s("exp_done"), 1)

            def chunk_high(c):
                act.wait_ge(stage_in[c % 2], 16 * (c // 2 + 1))
                raw, hi, _ = chunk(c)
                nc.scalar.activation(hi, raw, ACT.Copy).then_inc(s("chunk_hi"), 1)

            def moe_high(q, slot, free):
                act.wait_ge(raw_in[slot % 2], raw_count(q, slot))
                for b, count in enumerate(free):
                    if count is not None:
                        act.wait_ge(s(f"mdown{b}"), count)
                nc.scalar.activation(mw(wsm_hi, slot), raw_slot(slot % 2), ACT.Copy).then_inc(s("moe_hi"), 1)

            def raw_count(q, slot):
                if isinstance(q, int):
                    return 16 * (q // 2 + 1)
                return (q - slot % 2) * 8 + 16

            def moe_silu(b, j, i):
                table(SILU_SET)
                act.wait_ge(s(f"mg_psum{b}"), i + 1)
                nc.scalar.activation(W[b][1][:, j, :], PS[2 * b + 1][:, 0, :], ACT.Silu).then_inc(s(f"msilu{b}"), 1)

            def moe_hid(b, j, i, first=False):
                act.wait_ge(s(f"mgated{b}"), i + 1)
                if not first:
                    act.wait_ge(s(f"mdown{b}"), i - 1)
                nc.scalar.activation(a_hi[b][:, j, :], W[b][3][:, j, :], ACT.Copy).then_inc(s(f"mhi{b}"), 1)

            def moe(b, j, i, first=False):
                moe_silu(b, j, i)
                moe_hid(b, j, i, first)

            def lead_high(b, t):
                if t == 0:
                    act.wait_ge(s("wo_psum"), KC * NB)
                moe_high(t, t % SLOTS, (t - 3 if t > SLOTS - 1 else None,))

            steps = {
                "wsm": wsm_high, "chunk": chunk_high, "shift": shift, "h1": h1, "gate": gate, "q": q, "k": k,
                "xconv": xconv, "v": v, "ig": ig, "ga": ga, "og": og, "rk": rk, "rv": rv, "sqm": sqm, "rm": rm,
                "sqo": sqo, "ro": ro, "gated": gated, "wo": wo, "h2": h2, "silu": silu, "hid": hid, "acc": acc,
                "h3": h3, "exp": exp, "ehigh": lead_high, "esilu": lambda b, i: moe_silu(b, i % 2, i),
                "ehid": lambda b, i: moe_hid(b, i % 2, i, first=i < 2),
            }
            for name, args in plan(SCALAR_PLAN):
                steps[name](*args)

            def sum_out(b):
                act.wait_ge(s(f"mdown{b}"), NM)
                for c in range(KC):
                    nc.scalar.activation(W[b][0][:, c, :], PS[2 * b][:, c, :], ACT.Copy).then_inc(s("msum_sb"), 1)

            moe_high(LEAD + 2, (LEAD + 2) % SLOTS, (LEAD - 1,))
            moe(0, LEAD % 2, LEAD)
            moe(1, LEAD % 2, 0, first=True)
            with act.Fori(0, (NM - LEAD - 1) // SLOTS) as it:
                for jj in range(SLOTS):
                    q = it * SLOTS + (LEAD + 1 + jj)
                    slot = (LEAD + 1 + jj) % SLOTS
                    moe(0, slot % 2, q)
                    moe_high(q + 2, (slot + 2) % SLOTS, (q,))
                    moe(1, slot % 2, it * SLOTS + 1 + jj)
            for q in range(NM, NQ):
                if q + 2 < NQ:
                    moe_high(q + 2, (q + 2) % SLOTS, (None, q - 2 - LEAD + 1))
                moe(1, q % 2, q - LEAD)
                if q == NM:
                    sum_out(0)
            sum_out(1)

        @block.vector
        def _(dve):
            n = [0]

            def done(ins):
                ins.then_inc(s("dve_order"), 1)
                n[0] += 1
                return n[0]

            def link(ins):
                dve.wait_ge(s("dve_order"), done(ins))

            def stats(b, rows, ready):
                for t in range(NT):
                    at = done(nc.vector.bn_stats(st[b][:, t, :], rows[:, t, :]))
                dve.wait_ge(s("dve_order"), at)
                for t in range(NT):
                    last = nc.vector.bn_aggr(mv[b][:, t, :], st[b][:, t, :])
                last.then_inc(s(ready), 1)

            def normalise(b, dst, rows):
                for t in range(NT):
                    last = nc.vector.tensor_scalar(dst[:, t, :], rows[:, t, :], mv[b][:, t, 0:1], rr[b][:, t:t + 1],
                                                   ALU.subtract, ALU.mult)
                return last

            def per_token(b, i):
                return mod[:, b, i, :].unsqueeze(1).broadcast_to([P, NT, C])

            dve.wait_ge(s("const_ready"), 1)
            dve.wait_ge(s("cs_ready"), 1)
            nc.vector.tensor_copy(cB[:, :, :], cs[:, :].unsqueeze(2).broadcast_to([P, KC * NB, P])).then_inc(s("cB_ready"), 1)

            def minus_high(lo, full, hi, c, given, b, ready):
                dve.wait_ge(s(given), KC * b + c + 1)
                nc.vector.tensor_tensor(lo[:, c, :], full, f32(hi[:, c, :]), ALU.subtract).then_inc(s(ready), 1)

            def var0(b):
                dve.wait_ge(x_in[b], 16)
                stats(b, tok(W[b][0]), "var0")

            at = {}

            def scaled0(b):
                dve.wait_ge(s("mod_shift_sb"), b + 1)
                dve.wait_ge(s("var0"), b + 1)
                for t in range(NT):
                    at["scaled", b] = done(nc.vector.scalar_tensor_tensor(
                        tok(W[b][1])[:, t, :], tok(W[b][0])[:, t, :], mv[b][:, t, 0:1], mod[:, b, 1, :],
                        ALU.subtract, ALU.mult))

            def shifted(b):
                dve.wait_ge(s("rstd0"), b + 1)
                dve.wait_ge(s("dve_order"), at["scaled", b])
                for t in range(NT):
                    at["shifted", b] = done(nc.vector.scalar_tensor_tensor(
                        hm[b][:, t, :], tok(W[b][1])[:, t, :], rr[b][:, t:t + 1], mod[:, b, 0, :],
                        ALU.mult, ALU.add))

            def var1(b):
                dve.wait_ge(s("dve_order"), at["shifted", b])
                stats(b, hm[b], "var1")

            def hn1(b):
                dve.wait_ge(s("rstd1"), b + 1)
                normalise(b, tok(W[b][1]), hm[b]).then_inc(s("hn_ready"), 1)

            def vsum():
                dve.wait_ge(wsm_in[MATS.index("v") // 2], 16)
                vw = v_raw.rearrange("p k (h d) -> p k h d", d=HD)
                link(nc.vector.tensor_reduce(vmean[:, :].rearrange("p (k h) -> p k h", k=KC), vw, AX.X, ALU.add))
                nc.vector.tensor_scalar(vmean[:, :], vmean[:, :], 1.0 / HD, None, ALU.mult).then_inc(s("vsum_ready"), 1)

            def scaled():
                dve.wait_ge(s("par_in"), 16)
                nc.vector.tensor_scalar(half[:, :], par_sb[:, :], 0.5, None, ALU.mult).then_inc(s("par_half"), 1)
                dve.wait_ge(s("mats_in"), 16)
                nc.vector.tensor_scalar(blk_eps[:, :], blk, EPS * HD, None, ALU.mult).then_inc(s("blk_eps_ready"), 1)

            def modc_():
                dve.wait_ge(s("mod_chan"), 1)
                part = PA(0)[:, 0, 0:2 * KC * NB].rearrange("p (j b) -> p j b", b=NB)
                nc.vector.tensor_copy(modc[:, 0:KC, :], part[:, 0:KC, :])
                nc.vector.tensor_scalar(modc[:, KC:2 * KC, :], part[:, KC:2 * KC, :], 1.0, None,
                                        ALU.add).then_inc(s("modc_ready"), 1)

            def h1lo(b):
                for c in range(KC):
                    minus_high(a_lo[b], hpad[b][:, c, PAD:PAD + T], a_hi[b], c, "h1_full", b, "h1_lo")

            def conv(b, c):
                acc_ = W[b][0][:, c, :]
                link(nc.vector.tensor_scalar(acc_, hpad[b][:, c, 0:T], col("cw0", c), col("cb", c),
                                             ALU.mult, ALU.add))
                for k in range(1, KCONV):
                    ins = nc.vector.scalar_tensor_tensor(acc_, hpad[b][:, c, k:k + T], col(f"cw{k}", c), acc_,
                                                         ALU.mult, ALU.add)
                    if k < KCONV - 1:
                        link(ins)
                    else:
                        ins.then_inc(s("conv_ready"), 1)

            def xlo(b):
                for c in range(KC):
                    minus_high(b_lo[b], W[b][0][:, c, :], b_hi[b], c, "x_hi", b, "x_lo")

            def a1(b):
                for c in range(KC):
                    dve.wait_ge(s("sqk_ready"), KC * b + c + 1)
                    dve.wait_ge(s("ig_tanh"), KC * b + c + 1)
                    nc.vector.scalar_tensor_tensor(W[b][2][:, c, :], W[b][0][:, c, :], 1.0, W[b][2][:, c, :],
                                                   ALU.add, ALU.mult).then_inc(s("a1_done"), 1)

            def gamma(b):
                dve.wait_ge(s("ga_tanh"), KC * (b + 1))
                nc.vector.tensor_scalar(hpad[b][:, :, 0:T], hpad[b][:, :, 0:T], 0.5, 0.5,
                                        ALU.mult, ALU.add).then_inc(s("gamma_ready"), 1)

            def modg(b):
                if b:
                    dve.wait_ge(s("modg_ready"), b)
                dve.wait_ge(s("mod_gate_sb"), b + 1)
                g = mod[:, b, 2:4, :]
                link(nc.vector.tensor_scalar(gtmp[:, :, :], g, 0.0, 2.0, ALU.is_ge, ALU.mult))
                link(nc.vector.tensor_scalar(gtmp[:, :, :], gtmp[:, :, :], -1.0, None, ALU.add))
                link(nc.vector.tensor_tensor(g, g, gtmp[:, :, :], ALU.mult))
                nc.vector.scalar_tensor_tensor(g, g, 0.25, gtmp[:, :, :], ALU.max, ALU.mult).then_inc(s("modg_ready"), 1)

            def uk(b):
                for c in range(KC):
                    dve.wait_ge(s("a1_done"), KC * b + c + 1)
                    dve.wait_ge(s("rk_ready"), KC * b + c + 1)
                    done(nc.vector.tensor_tensor(W[b][2][:, c, :], W[b][2][:, c, :], W[b][5][:, c, :], ALU.mult))

            def uv(b):
                for c in range(KC):
                    dve.wait_ge(s("rv_ready"), KC * b + c + 1)
                    at["uv", b, c] = done(nc.vector.scalar_tensor_tensor(
                        W[b][3][:, c, :], W[b][3][:, c, :], col("vnw"), W[b][6][:, c, :], ALU.mult, ALU.mult))
                for c in range(KC):
                    dve.wait_ge(s("dve_order"), at["uv", b, c])
                    nc.vector.scalar_tensor_tensor(W[b][3][:, c, :], W[b][3][:, c, :], col("vnb"), W[b][2][:, c, :],
                                                   ALU.add, ALU.mult).then_inc(s("u_ready"), 1)

            def mem(b):
                dve.wait_ge(s("gamma_ready"), b + 1)
                for c in range(KC):
                    dve.wait_ge(s("uc_psum"), KC * b + c + 1)
                    nc.vector.tensor_tensor_scan(W[b][3][:, c, :], hpad[b][:, c, 0:T], PB(b)[:, c, :], 0.0,
                                                 ALU.mult, ALU.add).then_inc(s("mem_ready"), 1)

            def o1(b):
                at = [0] * KC
                for c in range(KC):
                    dve.wait_ge(s("rm_ready"), KC * b + c + 1)
                    at[c] = done(nc.vector.scalar_tensor_tensor(W[b][3][:, c, :], W[b][3][:, c, :], col("mnw"),
                                                                W[b][5][:, c, :], ALU.mult, ALU.mult))
                    dve.wait_ge(s("dve_order"), at[c])
                    nc.vector.scalar_tensor_tensor(W[b][3][:, c, :], W[b][3][:, c, :], col("mnb"), W[b][1][:, c, :],
                                                   ALU.add, ALU.mult).then_inc(s("o1_ready"), 1)

            def osig(b):
                dve.wait_ge(s("og_tanh"), KC * (b + 1))
                done(nc.vector.tensor_scalar(W[b][0][:, :, :], W[b][0][:, :, :], 0.5, 0.5, ALU.mult, ALU.add))

            def gated(b):
                at = [0] * KC
                for c in range(KC):
                    dve.wait_ge(s("ro_ready"), KC * b + c + 1)
                    at[c] = done(nc.vector.scalar_tensor_tensor(W[b][2][:, c, :], PB(b)[:, c, :], col("gnw", c),
                                                                W[b][6][:, c, :], ALU.mult, ALU.mult))
                    dve.wait_ge(s("dve_order"), at[c])
                    nc.vector.scalar_tensor_tensor(W[b][2][:, c, :], W[b][2][:, c, :], col("gnb", c),
                                                   W[b][0][:, c, :], ALU.add, ALU.mult).then_inc(s("gated"), 1)

            def outlo(b):
                for c in range(KC):
                    minus_high(a_lo[b], W[b][2][:, c, :], a_hi[b], c, "out_hi", b, "out_lo")

            def wo(b):
                dve.wait_ge(s("tw_psum"), b + 1)
                nc.vector.tensor_tensor(hm[b][:, :, :], hm[b][:, :, :], tok(PB(b)), ALU.add).then_inc(s("tw_used"), 1)

            def var2(b):
                dve.wait_ge(s("tw_used"), b + 1)
                stats(b, hm[b], "var2")

            def hn2(b):
                dve.wait_ge(s("rstd2"), b + 1)
                normalise(b, tok(W[b][1]), hm[b]).then_inc(s("hn2_ready"), 1)

            def h2lo(b):
                for c in range(KC):
                    minus_high(b_lo[b], W[b][3][:, c, :], b_hi[b], c, "h2_full", b, "h2_lo")

            def prod(b, f):
                i = b * NF + f
                dve.wait_ge(s("v2_psum"), i + 1)
                dve.wait_ge(s("silu_done"), i + 1)
                nc.vector.tensor_tensor(W[b][2][:, f % 2, :], W[b][1][:, f % 2, :], PA(b)[:, 1, :],
                                        ALU.mult).then_inc(s("prod_done"), 1)

            def hidlo(b, f):
                i = b * NF + f
                dve.wait_ge(s("hid_hi"), i + 1)
                nc.vector.tensor_tensor(a_lo[b][:, f % 2, :], W[b][2][:, f % 2, :], f32(a_hi[b][:, f % 2, :]),
                                        ALU.subtract).then_inc(s("hid_lo"), 1)

            def sum3(b):
                dve.wait_ge(s("tm_psum"), b + 1)
                nc.vector.tensor_tensor(hm[b][:, :, :], hm[b][:, :, :], tok(PA(b)), ALU.add).then_inc(s("tm_used"), 1)

            def gated3(b):
                dve.wait_ge(s("tm_used"), b + 1)
                dve.wait_ge(s("modg_ready"), b + 1)
                at["gated3", b] = done(nc.vector.tensor_tensor(hm[b][:, :, :], hm[b][:, :, :], per_token(b, 2),
                                                               ALU.mult))

            def plus_x(b):
                dve.wait_ge(s("x_again"), 16 * (b + 1))
                dve.wait_ge(s("dve_order"), at["gated3", b])
                at["x", b] = done(nc.vector.tensor_tensor(hm[b][:, :, :], hm[b][:, :, :], tok(W[b][0]), ALU.add))

            def var3(b):
                dve.wait_ge(s("dve_order"), at["x", b])
                stats(b, hm[b], "var3")

            def hn3(b):
                dve.wait_ge(s("rstd3"), b + 1)
                normalise(b, tok(W[b][1]), hm[b]).then_inc(s("hn3_ready"), 1)

            def h3lo(b):
                for c in range(KC):
                    minus_high(b_lo[b], W[b][3][:, c, :], b_hi[b], c, "h3_full", b, "h3_lo")

            def lgsub(b):
                lg = tok(PA(b))[:, :, 0:NE]
                dve.wait_ge(s("lg_psum"), b + 1)
                for t in range(NT):
                    at = done(nc.vector.max(top8[b][:, t, :], lg[:, t, :]))
                dve.wait_ge(s("dve_order"), at)
                nc.vector.tensor_tensor(rep[b][:, :, 0:NE], lg, top8[b][:, :, 0:1].broadcast_to([P, NT, NE]),
                                        ALU.subtract).then_inc(s("lg_sub"), 1)

            def topk(b):
                dve.wait_ge(s("exp_done"), b + 1)
                link(nc.vector.tensor_reduce(sums[b][:, :], rep[b][:, :, 0:NE], AX.X, ALU.add))
                link(nc.vector.reciprocal(sums[b][:, :], sums[b][:, :]))
                link(nc.vector.tensor_tensor(sc[b][:, :, 0:NE], rep[b][:, :, 0:NE],
                                             sums[b][:, :].unsqueeze(2).broadcast_to([P, NT, NE]), ALU.mult))
                for t in range(NT):
                    at = done(nc.vector.max(top8[b][:, t, :], sc[b][:, t, 0:NE]))
                dve.wait_ge(s("dve_order"), at)
                link(nc.vector.tensor_copy(top8[b][:, :, TOPK:8], sc[b][:, :, NE:NE + 4]))
                for t in range(NT):
                    at = done(nc.vector.match_replace(rep[b][:, t, :], top8[b][:, t, :], sc[b][:, t, :], -1.0))
                dve.wait_ge(s("dve_order"), at)
                link(nc.vector.scalar_tensor_tensor(wres[b][:, :, :], rep[b][:, :, 0:NE], 0.0, sc[b][:, :, 0:NE],
                                                    ALU.is_lt, ALU.mult))
                w4 = wcat[b][:, :, :].rearrange("p t (g e) -> p t g e", e=NG)
                for g in range(3):
                    link(nc.vector.tensor_copy(wb[b][:, g, :, :], wres[b][:, :, :]))
                    last = nc.vector.tensor_copy(w4[:, :, g, 0:NE], wb[b][:, g, :, :])
                    if g < 2:
                        link(nc.vector.tensor_tensor(wres[b][:, :, :], wres[b][:, :, :], wb[b][:, g, :, :], ALU.subtract))
                last.then_inc(s("wcat_ready"), 1)

            def weights_out(b):
                dve.wait_ge(s("wt_psum"), b + 1)
                nc.vector.tensor_copy(wT[:, b, :], PB(b)[0:3 * NG, 0, :]).then_inc(s("wt_ready"), 1)

            def moe_gated(b, j, i):
                gate_bank, up_bank = PS[2 * b + 1][:, 0, :], PS[2 * b + 1][:, 1, :]
                dve.wait_ge(s(f"mu_psum{b}"), i + 1)
                dve.wait_ge(s(f"msilu{b}"), i + 1)
                nc.vector.tensor_tensor(W[b][2][:, j, :], W[b][1][:, j, :], up_bank, ALU.mult).then_inc(s(f"mprod{b}"), 1)
                dve.wait_ge(s(f"mprod{b}"), i + 1)
                dve.wait_ge(s(f"mw_psum{b}"), i + 1)
                nc.vector.tensor_tensor(W[b][3][:, j, :], W[b][2][:, j, :], gate_bank, ALU.mult).then_inc(s(f"mgated{b}"), 1)

            def moe_lo(b, j, i):
                dve.wait_ge(s(f"mhi{b}"), i + 1)
                nc.vector.tensor_tensor(a_lo[b][:, j, :], W[b][3][:, j, :], f32(a_hi[b][:, j, :]),
                                        ALU.subtract).then_inc(s(f"mlo{b}"), 1)

            def moe(b, j, i):
                moe_gated(b, j, i)
                moe_lo(b, j, i)

            steps = {
                "var0": var0, "scaled0": scaled0, "shifted": shifted, "var1": var1, "hn1": hn1, "vsum": vsum, "scaled": scaled, "modc": modc_,
                "h1lo": h1lo, "conv": conv, "xlo": xlo, "a1": a1, "gamma": gamma, "modg": modg, "uk": uk, "uv": uv, "mem": mem,
                "o1": o1, "osig": osig, "gated": gated, "outlo": outlo, "wo": wo, "var2": var2, "hn2": hn2, "h2lo": h2lo,
                "prod": prod, "hidlo": hidlo, "sum3": sum3, "gated3": gated3, "plus_x": plus_x, "var3": var3, "hn3": hn3, "h3lo": h3lo, "lgsub": lgsub, "topk": topk,
                "wt": weights_out, "egated": lambda b, i: moe_gated(b, i % 2, i), "elo": lambda b, i: moe_lo(b, i % 2, i),
            }
            for name, args in plan(VECTOR_PLAN):
                steps[name](*args)

            def finish(b):
                dve.wait_ge(s("mt_psum"), b + 1)
                link(nc.vector.tensor_tensor(tok(W[b][2]), tok(PS[2 * b + 1]), per_token(b, 3), ALU.mult))
                nc.vector.tensor_tensor(hm[b][:, :, :], hm[b][:, :, :], tok(W[b][2]), ALU.add).then_inc(s("y_ready"), 1)

            moe(0, LEAD % 2, LEAD)
            moe(1, LEAD % 2, 0)
            with dve.Fori(0, (NM - LEAD - 1) // 2) as it:
                for jj in range(2):
                    moe(0, (LEAD + 1 + jj) % 2, it * 2 + (LEAD + 1 + jj))
                    moe(1, (LEAD + 1 + jj) % 2, it * 2 + (1 + jj))
            for q in range(NM, NQ):
                moe(1, q % 2, q - LEAD)
                if q == NM + 1:
                    finish(0)
            finish(1)

        @block.tensor
        def _(pe):
            mm = nc.tensor.matmul

            def product(out, w_hi, w_lo, r_hi, r_lo, hi_in, lo_in, ready, start=True, stop=True, by_k=False):
                kk = range(len(r_hi))

                def high(m, k):
                    mm(out(m), w_hi(k, m), r_hi[k], start=start and k == 0, stop=False)
                    mm(out(m), w_lo(k, m), r_hi[k], start=False, stop=False)

                if by_k:
                    for k in kk:
                        hi_in(k)
                        for m in range(KC):
                            high(m, k)
                for m in range(KC):
                    if not by_k:
                        for k in kk:
                            if m == 0:
                                hi_in(k)
                            high(m, k)
                    for k in kk:
                        if m == 0:
                            lo_in(k)
                        last = mm(out(m), w_hi(k, m), r_lo[k], start=False, stop=stop and k == kk[-1])
                    if ready:
                        last.then_inc(s(ready), 1)
                return last

            def small(name, b, out, hi, lo, hi_ready, lo_ready, ready, by_k=False):
                pe.wait_ge(s("wsm_ready"), MATS.index(name) + 1)
                product(lambda m: out[:, m, :], lambda k, m: mat(wsm_hi, name, k, m),
                        lambda k, m: mat(wsm_lo, name, k, m),
                        [hi[:, k, :] for k in range(KC)], [lo[:, k, :] for k in range(KC)],
                        lambda k: pe.wait_ge(s(hi_ready), KC * b + k + 1),
                        lambda k: pe.wait_ge(s(lo_ready), KC * b + k + 1), ready, by_k=by_k)

            def to_channels(out, rows):
                for c in range(KC):
                    for t in range(NT):
                        last = nc.tensor.transpose(out[:, c, t * P:(t + 1) * P], rows[:, t, c * P:(c + 1) * P], ident)
                return last

            def to_tokens(out, chans, given):
                for c in range(KC):
                    given(c)
                    for t in range(NT):
                        last = nc.tensor.transpose(out[:, t, c * P:(c + 1) * P], chans[:, c, t * P:(t + 1) * P], ident)
                return last

            cB4 = cB[:, :, :].rearrange("p (k b) m -> p k b m", b=NB)

            def shift(b):
                pe.wait_ge(s("cB_ready"), 1)
                pe.wait_ge(wmod_in[0], 16)
                for k in range(KC):
                    last = mm(PA(b)[:, 0, :], cB4[:, k, b, :], wmod_raw[0][:, k, :], start=k == 0, stop=k == KC - 1)
                last.then_inc(s("mod_shift"), 1)

            def t1(b):
                pe.wait_ge(s("mats_in"), 16)
                pe.wait_ge(s("hn_ready"), b + 1)
                to_channels(PB(b), tok(W[b][1])).then_inc(s("t1_psum"), 1)

            def modulation(b):
                pe.wait_ge(wmod_in[1], 16)
                pe.wait_ge(wmod_in[2], 16)
                if b == 0:
                    pe.wait_ge(s("mod_shift_sb"), 1)
                    for j in range(2 * KC):
                        part = wmod_raw[1][:, :, C + j * P:C + (j + 1) * P] if j < KC else \
                            wmod_raw[2][:, :, (j - KC) * P:(j - KC + 1) * P]
                        for k in range(KC):
                            last = mm(PA(0)[:, 0, j * NB:(j + 1) * NB], part[:, k, :], cs[:, k * NB:(k + 1) * NB],
                                      start=k == 0, stop=k == KC - 1)
                    last.then_inc(s("mod_chan"), 1)
                for g, part in enumerate((wmod_raw[1][:, :, 0:C], wmod_raw[2][:, :, C:2 * C])):
                    for k in range(KC):
                        last = mm(PA(b)[:, 1, g * C:(g + 1) * C], cB4[:, k, b, :], part[:, k, :],
                                  start=k == 0, stop=k == KC - 1)
                last.then_inc(s("mod_gate"), 1)

            def q(b):
                pe.wait_ge(s("mod_gate_sb"), b + 1)
                pe.wait_ge(s("modc_ready"), 1)
                small("q", b, PA(b), a_hi[b], a_lo[b], "h1_full", "h1_lo", "q_psum", by_k=True)

            def k(b):
                small("k", b, PB(b), a_hi[b], a_lo[b], "h1_full", "h1_lo", "k_psum")

            def v(b):
                pe.wait_ge(s("q_used"), KC * (b + 1))
                small("v", b, PA(b), a_hi[b], a_lo[b], "h1_full", "h1_lo", "v_psum")

            def ig(b):
                pe.wait_ge(s("k_used"), KC * (b + 1))
                small("ig", b, PB(b), b_hi[b], b_lo[b], "x_hi", "x_lo", "ig_psum", by_k=True)

            def ga(b):
                pe.wait_ge(s("v_used"), KC * (b + 1))
                small("ga", b, PA(b), b_hi[b], b_lo[b], "x_hi", "x_lo", "ga_psum")

            def ssk(b):
                for c in range(KC):
                    pe.wait_ge(s("ig_tanh"), KC * b + c + 1)
                    pe.wait_ge(s("sqk_ready"), KC * b + c + 1)
                    mm(PB(b)[:, c, :], blk, W[b][5][:, c, :], start=True, stop=True).then_inc(s("ssk_psum"), 1)

            def og(b):
                pe.wait_ge(s("ga_tanh"), KC * (b + 1))
                small("og", b, PA(b), b_hi[b], b_lo[b], "x_hi", "x_lo", "og_psum")

            def ssv(b):
                for c in range(KC):
                    pe.wait_ge(s("og_tanh"), KC * b + c + 1)
                    pe.wait_ge(s("sqv_ready"), KC * b + c + 1)
                    mm(PA(b)[:, c, :], blk, W[b][6][:, c, :], start=True, stop=True).then_inc(s("ssv_psum"), 1)

            def u(b):
                for c in range(KC):
                    pe.wait_ge(s("rk_ready"), KC * b + c + 1)
                    pe.wait_ge(s("u_ready"), KC * b + c + 1)
                    mm(PB(b)[:, c, :], cen, W[b][3][:, c, :], start=True, stop=True).then_inc(s("uc_psum"), 1)

            def mem(b):
                for c in range(KC):
                    pe.wait_ge(s("rv_ready"), KC * b + c + 1)
                    pe.wait_ge(s("sqm_ready"), KC * b + c + 1)
                    mm(PA(b)[:, c, :], blk, W[b][5][:, c, :], start=True, stop=True).then_inc(s("ssm_psum"), 1)

            def oc(b):
                for c in range(KC):
                    pe.wait_ge(s("mem_ready"), KC * b + c + 1)
                    pe.wait_ge(s("o1_ready"), KC * b + c + 1)
                    mm(PB(b)[:, c, :], cen, W[b][3][:, c, :], start=True, stop=True).then_inc(s("oc_psum"), 1)

            def vo(b):
                pe.wait_ge(s("blk_eps_ready"), 1)
                for c in range(KC):
                    pe.wait_ge(s("sqq_ready"), KC * b + c + 1)
                    pe.wait_ge(s("rm_ready"), KC * b + c + 1)
                    mm(PA(b)[:, c, :], blk_eps[:, :], W[b][4][:, c, :], start=True, stop=False)
                    pe.wait_ge(s("sqo_ready"), KC * b + c + 1)
                    mm(PA(b)[:, c, :], blk, W[b][6][:, c, :], start=False, stop=True).then_inc(s("vo_psum"), 1)

            def wo(b):
                pe.wait_ge(s("ro_ready"), KC * (b + 1))
                small("o", b, PA(b), a_hi[b], a_lo[b], "out_hi", "out_lo", "wo_psum", by_k=True)

            def tw(b):
                pe.wait_ge(s("gated"), KC * (b + 1))
                to_tokens(tok(PB(b)), W[b][3],
                          lambda c: pe.wait_ge(s("wo_sb"), KC * b + c + 1)).then_inc(s("tw_psum"), 1)

            def t2(b):
                pe.wait_ge(s("hn2_ready"), b + 1)
                to_channels(PA(b), tok(W[b][1])).then_inc(s("t2_psum"), 1)

            def ff_down(b, f):
                i = b * NF + f
                pe.wait_ge(s("chunk_split"), NCH_FF + 1 + f // 4)
                product(lambda m: PB(b)[:, m, :], lambda k, m: wout_hi[:, f, m * P:(m + 1) * P],
                        lambda k, m: wout_lo[:, f, m * P:(m + 1) * P],
                        [a_hi[b][:, f % 2, :]], [a_lo[b][:, f % 2, :]],
                        lambda k: pe.wait_ge(s("hid_hi"), i + 1), lambda k: pe.wait_ge(s("hid_lo"), i + 1),
                        None, start=f == 0, stop=f == NF - 1, by_k=True).then_inc(s("down_done"), 1)

            def half_ff(b, f, which, ready):
                o = (2 * f + which) * P
                out = PA(b)[:, which, :]
                for k in range(KC):
                    mm(out, wff_hi[:, k, o:o + P], b_hi[b][:, k, :], start=k == 0, stop=False)
                    mm(out, wff_lo[:, k, o:o + P], b_hi[b][:, k, :], start=False, stop=False)
                if f == 0 and which == 0:
                    pe.wait_ge(s("h2_lo"), KC * (b + 1))
                for k in range(KC):
                    last = mm(out, wff_hi[:, k, o:o + P], b_lo[b][:, k, :], start=False, stop=k == KC - 1)
                last.then_inc(s(ready), 1)

            def ff_up(b, f):
                i = b * NF + f
                pe.wait_ge(s("chunk_split"), 1 + f // 2)
                if f == 0:
                    pe.wait_ge(s("h2_full"), KC * (b + 1))
                    pe.wait_ge(s("tw_used"), b + 1)
                else:
                    pe.wait_ge(s("silu_done"), i)
                half_ff(b, f, 0, "g_psum")
                if f:
                    pe.wait_ge(s("prod_done"), i)
                half_ff(b, f, 1, "v2_psum")

            def tm(b):
                to_tokens(tok(PA(b)), W[b][3],
                          lambda c: pe.wait_ge(s("acc_sb"), KC * b + c + 1)).then_inc(s("tm_psum"), 1)

            def t3(b):
                pe.wait_ge(s("hn3_ready"), b + 1)
                to_channels(PB(b), tok(W[b][1])).then_inc(s("t3_psum"), 1)

            def logits(b):
                pe.wait_ge(s("wg_in"), 16)
                pe.wait_ge(s("h3_full"), KC * (b + 1))
                pe.wait_ge(s("tm_used"), b + 1)
                for t in range(NT):
                    for k in range(KC):
                        last = mm(tok(PA(b))[:, t, 0:NE], W[b][3][:, k, t * P:(t + 1) * P], wg_sb[:, k, :],
                                  start=k == 0, stop=k == KC - 1)
                last.then_inc(s("lg_psum"), 1)

            def weights_out(b):
                pe.wait_ge(s("wcat_ready"), b + 1)
                for t in range(NT):
                    last = nc.tensor.transpose(PB(b)[0:3 * NG, 0, t * P:(t + 1) * P], wcat[b][:, t, :], ident)
                last.then_inc(s("wt_psum"), 1)

            def moe_half(b, slot, which, before_last=None):
                bank = PS[2 * b + 1][:, which, :]
                for k in range(KC):
                    mm(bank, mgu(wsm_hi, slot, k, which), b_hi[b][:, k, :], start=k == 0, stop=False)
                    mm(bank, mgu(wsm_lo, slot, k, which), b_hi[b][:, k, :], start=False, stop=False)
                    if k == KC - 1 and before_last:
                        before_last()
                    last = mm(bank, mgu(wsm_hi, slot, k, which), b_lo[b][:, k, :], start=False, stop=k == KC - 1)
                return last

            def moe_up(b, slot, i, tile, passing, first=False):
                pe.wait_ge(s("moe_ready"), passing + 1)
                if not first:
                    pe.wait_ge(s(f"mgated{b}"), i)
                moe_half(b, slot, 0).then_inc(s(f"mg_psum{b}"), 1)
                moe_half(b, slot, 1, lambda: pe.wait_ge(s(f"msilu{b}"), i + 1)).then_inc(s(f"mu_psum{b}"), 1)
                mm(PS[2 * b + 1][:, 0, :], sel_bf[:, bass.ts(tile, P)], wT[:, b, :],
                   start=True, stop=True).then_inc(s(f"mw_psum{b}"), 1)

            def moe_down(b, slot, j, i, start=False, stop=False):
                pe.wait_ge(s(f"mhi{b}"), i + 1)
                for m in range(KC):
                    mm(PS[2 * b][:, m, :], mdn(wsm_hi, slot, m), a_hi[b][:, j, :], start=start, stop=False)
                    mm(PS[2 * b][:, m, :], mdn(wsm_lo, slot, m), a_hi[b][:, j, :], start=False, stop=False)
                pe.wait_ge(s(f"mlo{b}"), i + 1)
                for m in range(KC):
                    last = mm(PS[2 * b][:, m, :], mdn(wsm_hi, slot, m), a_lo[b][:, j, :], start=False, stop=stop)
                last.then_inc(s(f"mdown{b}"), 1)

            def lead_up(b, t):
                if t == 0:
                    pe.wait_ge(s("h3_lo"), KC)
                    pe.wait_ge(s("wt_ready"), 1)
                    pe.wait_ge(s("chunk_split"), len(CH))
                moe_up(0, t % SLOTS, t, t, t, first=t == 0)

            def lead_down(b, t):
                moe_down(0, t % SLOTS, t % 2, t, start=t == 0)

            steps = {
                "shift": shift, "t1": t1, "modulation": modulation, "q": q, "k": k, "v": v, "ig": ig, "ga": ga,
                "ssk": ssk, "og": og, "ssv": ssv, "u": u, "mem": mem, "oc": oc, "vo": vo, "wo": wo, "tw": tw, "t2": t2,
                "up": ff_up, "down": ff_down, "tm": tm, "t3": t3, "logits": logits, "wt": weights_out,
                "eup": lead_up, "edown": lead_down,
            }
            for name, args in plan(TENSOR_PLAN):
                steps[name](*args)

            moe_up(0, LEAD % SLOTS, LEAD, LEAD, LEAD)
            moe_down(0, (LEAD - 1) % SLOTS, (LEAD - 1) % 2, LEAD - 1)
            pe.wait_ge(s("h3_lo"), KC * NB)
            pe.wait_ge(s("wt_ready"), NB)
            pe.wait_ge(s("zeros_ready"), 1)
            for m in range(KC):
                mm(PS[2][:, m, :], zeros[:, 0:P], zeros[:, :], start=True, stop=False)
            moe_up(1, LEAD % SLOTS, 0, LEAD, LEAD, first=True)
            with pe.Fori(0, (NM - LEAD - 1) // SLOTS) as it:
                for jj in range(SLOTS):
                    q = it * SLOTS + (LEAD + 1 + jj)
                    slot = (LEAD + 1 + jj) % SLOTS
                    before = (slot - 1) % SLOTS
                    moe_down(0, before, before % 2, it * SLOTS + (LEAD + jj))
                    moe_up(0, slot, q, q, q)
                    moe_down(1, before, before % 2, it * SLOTS + jj)
                    moe_up(1, slot, it * SLOTS + (1 + jj), q, q)
            moe_down(0, (NM - 1) % SLOTS, (NM - 1) % 2, NM - 1, stop=True)
            for q in range(NM, NQ):
                moe_up(1, q % SLOTS, q - LEAD, q - NM, q)
                moe_down(1, (q - 1) % SLOTS, (q - 1) % 2, q - 1 - LEAD)
                if q == NM + 1:
                    to_tokens(tok(PS[1]), W[0][0], lambda c: pe.wait_ge(s("msum_sb"), c + 1)).then_inc(s("mt_psum"), 1)
            moe_down(1, (NQ - 1) % SLOTS, (NQ - 1) % 2, NM - 1, stop=True)
            to_tokens(tok(PS[3]), W[1][0], lambda c: pe.wait_ge(s("msum_sb"), KC + c + 1)).then_inc(s("mt_psum"), 1)


def kernel(**inputs):
    import numpy as np
    import concourse.bacc as bacc
    from concourse.bass_utils import run_bass_kernel_spmd

    a = {k.replace("L0_", ""): np.asarray(v) for k, v in inputs.items()}
    f = np.float32

    def rows(w):
        return np.ascontiguousarray(w.reshape(-1, P, w.shape[1]).transpose(1, 0, 2))

    per_channel = {
        "ln1w": a["attn_ln1w"], "ln1b": a["attn_ln1b"], "cb": a["attn_conv_b"], "big": a["attn_big"],
        "bg": np.repeat(a["attn_bg"], HD), "bog": a["attn_bog"], "gnw": a["attn_gnw"], "gnb": a["attn_gnb"],
        "ln2w": a["attn_ln2w"], "ln2b": a["attn_ln2b"],
        **{f"cw{k}": a["attn_conv_w"][:, 0, k] for k in range(KCONV)},
    }
    par = np.concatenate([per_channel[n].reshape(KC, P).T for n in COLS]
                         + [np.tile(a["attn_" + n], P // HD)[:, None] for n in ONCE], axis=1)
    wsm = rows(np.concatenate([a["attn_Wq"], a["attn_Wk"], a["attn_Wig"], a["attn_Wv"],
                               np.repeat(a["attn_Wg"], HD, axis=1), a["attn_Wog"], a["attn_Wo"]], axis=1))
    gv = np.stack([a["attn_Wgate"].reshape(C, NF, P), a["attn_Wval"].reshape(C, NF, P)], axis=2)
    wff = rows(gv.reshape(C, 2 * FF))
    wout = rows(a["attn_Wout"])
    gu, sg = a["ffn_gate_up_weights"], a["ffn_shared_gate_up"]
    fill = NM * P - HIDDEN
    gate = np.concatenate([gu[:, :FE].reshape(-1, C), sg[:2 * FE], np.zeros((fill, C), f)])
    up = np.concatenate([gu[:, FE:].reshape(-1, C), sg[2 * FE:], np.zeros((fill, C), f)])
    down = np.concatenate([a["ffn_down_weights"].transpose(0, 2, 1).reshape(-1, C), a["ffn_shared_down"].T,
                           np.zeros((fill, C), f)])
    g = np.stack([gate, up]).reshape(2, NM, P, KC, P).transpose(1, 4, 3, 0, 2).reshape(NM, P, 2 * KC * P)
    wmoe = np.concatenate([g, down.reshape(NM, P, C)], axis=2)
    unit = np.minimum(np.arange(NM * P) // FE, NE)
    sel = np.tile((unit[None, :] == np.arange(NG)[:, None]).astype(f), (3, 1))
    head = np.arange(P) // HD
    block_mean = ((head[:, None] == head[None, :]) / HD).astype(f)
    mats = np.stack([np.eye(P, dtype=f), block_mean, np.eye(P, dtype=f) - block_mean], axis=1)

    arrays = {
        "x": a["attn_x"].reshape(NB * T, C),
        "cT": a["c"].T.reshape(KC, P, NB).transpose(1, 0, 2).reshape(P, KC * NB),
        "wmod": rows(a["wmod"]), "par": par, "wsm": wsm, "wff": wff, "wout": wout,
        "wgate": rows(np.ascontiguousarray(a["ffn_gate_weight"].T)), "wmoe": wmoe, "sel": sel, "mats": mats,
    }
    arrays = {"in_" + k: np.ascontiguousarray(v) for k, v in arrays.items()}
    nc = bacc.Bacc("TRN2", target_bir_lowering=False, num_devices=1, dynamic_dma_scratch_size=1024)
    args = [nc.dram_tensor(k, v.shape, FP32, kind="ExternalInput").ap() for k, v in arrays.items()]
    args.append(nc.dram_tensor("out", (NB * T, C), FP32, kind="ExternalOutput").ap())
    adaln_block_kernel(nc, *args)
    r = run_bass_kernel_spmd(nc, [arrays], core_ids=[0])
    return np.asarray(r.results[0]["out"]).reshape(NB, T, C)
```
